# Optimizing a Trainium2 kernel written in Bass

```python
import numpy as np
import jax
import jax.numpy as jnp

def _softmax(x, axis=-1):
    return jax.nn.softmax(x, axis=axis)

def _gelu(x):
    return jax.nn.gelu(x, approximate=True)

def _silu(x):
    return jax.nn.silu(x)

def _sigmoid(x):
    return jax.nn.sigmoid(x)

def _layernorm(x, axis=-1, eps=1e-05):
    m = jnp.mean(x, axis=axis, keepdims=True)
    v = jnp.var(x, axis=axis, keepdims=True)
    return (x - m) / jnp.sqrt(v + eps)

def _scatter_add(tgt, idx, src, axis=0):
    return tgt.at[idx].add(src)

def _segment_sum(src, seg, n):
    return jax.ops.segment_sum(src, seg, n)
kernel_name = 'mk_gnn_resnorm_d4_gnn_r8_312bdf'

def setup_inputs(seed: int=0):
    np.random.seed(seed)
    _w = jnp.asarray

    def _rec_inputs():
        import jax
        import jax.numpy as jnp
        _gk = jax.random.key(seed)
        x = -0.0005121 + 1.001 * jax.random.normal(jax.random.fold_in(_gk, 1), (12500, 64), jnp.float32)
        src = jax.random.randint(jax.random.fold_in(_gk, 2), (400000,), 0, 12500, jnp.int32)
        dst = jnp.minimum((12500 * jax.random.uniform(jax.random.fold_in(_gk, 3), (400000,)) ** 2.0).astype(jnp.int32), 99999)
        _o = jnp.argsort(dst, stable=True)
        src = src[_o]
        dst = dst[_o]
        edge_attr_16 = -9.77346e-05 + 0.999888 * jax.random.normal(jax.random.fold_in(_gk, 13), (400000, 16), jnp.float32)
        edge_attr_32 = 0.000189758 + 1.00013 * jax.random.normal(jax.random.fold_in(_gk, 14), (400000, 32), jnp.float32)
        edge_attr_64 = -9.77346e-05 + 0.999888 * jax.random.normal(jax.random.fold_in(_gk, 15), (400000, 64), jnp.float32)
        edge_type_16 = jax.random.randint(jax.random.fold_in(_gk, 17), (400000,), 0, 16, jnp.int32)
        return (x, src, dst, edge_attr_16, edge_attr_32, edge_attr_64, edge_type_16)
    x, src, dst, edge_attr_16, edge_attr_32, edge_attr_64, edge_type_16 = _rec_inputs()

    def _L0_gnn_setup():
        import jax, jax.numpy as jnp
        import numpy as np
        N_NODES = 6250
        N_EDGES = 100000
        D_NODE = 64
        D_EDGE = 64
        HIDDEN = 128
        key = jax.random.key(seed)
        k1, k2, k3, k4, k5 = jax.random.split(key, 5)
        x_node = jax.random.normal(k1, (N_NODES, D_NODE), dtype=jnp.float32)
        x_edge = jax.random.normal(k2, (N_EDGES, D_EDGE), dtype=jnp.float32)
        edge_index = jax.random.randint(k3, (2, N_EDGES), 0, N_NODES, dtype=jnp.int64)
        d_in = D_NODE + D_EDGE
        W1 = jax.random.normal(k4, (d_in, HIDDEN), dtype=jnp.float32) / np.sqrt(d_in)
        b1 = jnp.zeros((HIDDEN,), dtype=jnp.float32)
        W2 = jax.random.normal(k5, (HIDDEN, D_NODE), dtype=jnp.float32) / np.sqrt(HIDDEN)
        b2 = jnp.zeros((D_NODE,), dtype=jnp.float32)
        return {'x_node': x_node, 'x_edge': x_edge, 'edge_index': edge_index, 'W1': W1, 'b1': b1, 'W2': W2, 'b2': b2}
    _L0_gnn_all = _L0_gnn_setup()
    _L0_gnn_in = {k: v for k, v in _L0_gnn_all.items() if k in ('W1', 'b1', 'W2', 'b2')}
    del _L0_gnn_all

    def _L1_gnn_setup():
        import jax, jax.numpy as jnp
        import numpy as np
        N_NODES = 12500
        N_EDGES = 400000
        F_E, F_X, F_U, H, F_OUT = (16, 64, 64, 128, 64)
        N_GRAPHS = 64
        key = jax.random.key(seed)
        ks = jax.random.split(key, 8)
        x = jax.random.normal(ks[0], (N_NODES, F_X), dtype=jnp.float32)
        edge_attr = jax.random.normal(ks[1], (N_EDGES, F_E), dtype=jnp.float32)
        u = jax.random.normal(ks[2], (N_GRAPHS, F_U), dtype=jnp.float32)
        d_in = F_E + F_X + F_U
        W1 = jax.random.normal(ks[3], (d_in, H), dtype=jnp.float32) / np.sqrt(d_in)
        b1 = jnp.zeros((H,), dtype=jnp.float32)
        W2 = jax.random.normal(ks[4], (H, F_OUT), dtype=jnp.float32) / np.sqrt(H)
        b2 = jnp.zeros((F_OUT,), dtype=jnp.float32)
        edge_index = jax.random.randint(ks[5], (2, N_EDGES), 0, N_NODES, dtype=jnp.int64)
        batch = jnp.sort(jax.random.randint(ks[6], (N_NODES,), 0, N_GRAPHS, dtype=jnp.int64))
        return {'x': x, 'edge_attr': edge_attr, 'u': u, 'W1': W1, 'b1': b1, 'W2': W2, 'b2': b2, 'edge_index': edge_index, 'batch': batch}
    _L1_gnn_all = _L1_gnn_setup()
    _L1_gnn_in = {k: v for k, v in _L1_gnn_all.items() if k in ('u', 'W1', 'b1', 'W2', 'b2')}
    del _L1_gnn_all

    def _L2_gnn_setup():
        import jax, jax.numpy as jnp
        import numpy as np
        N_NODES = 6250
        N_EDGES = 100000
        D_IN = 64
        D_OUT = 64
        NUM_RELS = 16
        key = jax.random.key(seed)
        k1, k2, k3, k4, k5 = jax.random.split(key, 5)
        feat = jax.random.normal(k1, (N_NODES, D_IN), dtype=jnp.float32)
        weight = jax.random.normal(k2, (NUM_RELS, D_IN, D_OUT), dtype=jnp.float32) * 0.05
        src = jax.random.randint(k3, (N_EDGES,), 0, N_NODES, dtype=jnp.int32)
        dst = jax.random.randint(k4, (N_EDGES,), 0, N_NODES, dtype=jnp.int32)
        etypes = jax.random.randint(k5, (N_EDGES,), 0, NUM_RELS, dtype=jnp.int32)
        return {'feat': feat, 'weight': weight, 'src': src, 'dst': dst, 'etypes': etypes}
    _L2_gnn_all = _L2_gnn_setup()
    _L2_gnn_in = {k: v for k, v in _L2_gnn_all.items() if k in ('weight',)}
    del _L2_gnn_all

    def _L3_gnn_setup():
        import jax, jax.numpy as jnp
        import numpy as np
        N_NODES = 12500
        N_EDGES = 200000
        N_GRAPHS = 64
        NODE_IN = 64
        EDGE_IN = 32
        GLOBAL_IN = 32
        NODE_OUT = 64
        MSG = 32

        def _linear_params(key, fan_in, fan_out):
            kw, kb = jax.random.split(key)
            s = 1.0 / np.sqrt(fan_in)
            W = jax.random.uniform(kw, (fan_in, fan_out), jnp.float32, -s, s)
            b = jax.random.uniform(kb, (fan_out,), jnp.float32, -s, s)
            return (W, b)
        key = jax.random.key(seed)
        ks = jax.random.split(key, 12)
        x = jax.random.normal(ks[0], (N_NODES, NODE_IN), jnp.float32)
        edge_index = jax.random.randint(ks[1], (2, N_EDGES), 0, N_NODES, jnp.int64 if jax.config.jax_enable_x64 else jnp.int32)
        edge_attr = jax.random.normal(ks[2], (N_EDGES, EDGE_IN), jnp.float32)
        u = jax.random.normal(ks[3], (N_GRAPHS, GLOBAL_IN), jnp.float32)
        batch = jnp.sort(jax.random.randint(ks[4], (N_NODES,), 0, N_GRAPHS))
        W1, b1 = _linear_params(ks[5], 2 * NODE_IN + EDGE_IN, MSG)
        W2, b2 = _linear_params(ks[6], MSG, MSG)
        W3, b3 = _linear_params(ks[7], MSG, MSG)
        W4, b4 = _linear_params(ks[8], 2 * MSG + NODE_IN + GLOBAL_IN, MSG)
        W5, b5 = _linear_params(ks[9], MSG, MSG)
        W6, b6 = _linear_params(ks[10], MSG, NODE_OUT)
        return {'x': x, 'edge_index': edge_index, 'edge_attr': edge_attr, 'u': u, 'batch': batch, 'W1': W1, 'b1': b1, 'W2': W2, 'b2': b2, 'W3': W3, 'b3': b3, 'W4': W4, 'b4': b4, 'W5': W5, 'b5': b5, 'W6': W6, 'b6': b6}
    _L3_gnn_all = _L3_gnn_setup()
    _L3_gnn_in = {k: v for k, v in _L3_gnn_all.items() if k in ('u', 'W1', 'b1', 'W2', 'b2', 'W3', 'b3', 'W4', 'b4', 'W5', 'b5', 'W6', 'b6')}
    del _L3_gnn_all
    return {'x': x, 'src': src, 'dst': dst, 'edge_attr_16': edge_attr_16, 'edge_attr_32': edge_attr_32, 'edge_attr_64': edge_attr_64, 'edge_type_16': edge_type_16, 'L0_gnn_W1': _L0_gnn_in['W1'], 'L0_gnn_b1': _L0_gnn_in['b1'], 'L0_gnn_W2': _L0_gnn_in['W2'], 'L0_gnn_b2': _L0_gnn_in['b2'], 'L1_gnn_u': _L1_gnn_in['u'], 'L1_gnn_W1': _L1_gnn_in['W1'], 'L1_gnn_b1': _L1_gnn_in['b1'], 'L1_gnn_W2': _L1_gnn_in['W2'], 'L1_gnn_b2': _L1_gnn_in['b2'], 'L2_gnn_weight': _L2_gnn_in['weight'], 'L3_gnn_u': _L3_gnn_in['u'], 'L3_gnn_W1': _L3_gnn_in['W1'], 'L3_gnn_b1': _L3_gnn_in['b1'], 'L3_gnn_W2': _L3_gnn_in['W2'], 'L3_gnn_b2': _L3_gnn_in['b2'], 'L3_gnn_W3': _L3_gnn_in['W3'], 'L3_gnn_b3': _L3_gnn_in['b3'], 'L3_gnn_W4': _L3_gnn_in['W4'], 'L3_gnn_b4': _L3_gnn_in['b4'], 'L3_gnn_W5': _L3_gnn_in['W5'], 'L3_gnn_b5': _L3_gnn_in['b5'], 'L3_gnn_W6': _L3_gnn_in['W6'], 'L3_gnn_b6': _L3_gnn_in['b6']}

def reference(x, src, dst, edge_attr_16, edge_attr_32, edge_attr_64, edge_type_16, L0_gnn_W1, L0_gnn_b1, L0_gnn_W2, L0_gnn_b2, L1_gnn_u, L1_gnn_W1, L1_gnn_b1, L1_gnn_W2, L1_gnn_b2, L2_gnn_weight, L3_gnn_u, L3_gnn_W1, L3_gnn_b1, L3_gnn_W2, L3_gnn_b2, L3_gnn_W3, L3_gnn_b3, L3_gnn_W4, L3_gnn_b4, L3_gnn_W5, L3_gnn_b5, L3_gnn_W6, L3_gnn_b6):
    import jax
    import jax.numpy as jnp

    def _L0_gnn_ref(x_node, x_edge, edge_index, W1, b1, W2, b2):
        import jax, jax.numpy as jnp
        import numpy as np
        N_NODES = 6250
        N_EDGES = 100000
        D_NODE = 64
        D_EDGE = 64
        HIDDEN = 128
        agg = jnp.zeros((x_node.shape[0], x_edge.shape[1]), dtype=x_edge.dtype)
        agg = agg.at[edge_index[0]].add(x_edge)
        agg = agg.at[edge_index[1]].add(x_edge)
        h = jnp.concatenate([x_node, agg], axis=1)
        h = jax.nn.relu(h @ W1 + b1)
        x_node_ = h @ W2 + b2
        return x_node_

    def _L1_gnn_ref(x, edge_attr, u, W1, b1, W2, b2, edge_index, batch):
        import jax, jax.numpy as jnp
        import numpy as np
        N_NODES = 12500
        N_EDGES = 400000
        F_E, F_X, F_U, H, F_OUT = (16, 64, 64, 128, 64)
        N_GRAPHS = 64
        n_nodes = x.shape[0]
        col = edge_index[1]
        sums = jax.ops.segment_sum(edge_attr, col, num_segments=n_nodes)
        ones = jnp.ones((col.shape[0], 1), dtype=edge_attr.dtype)
        cnt = jax.ops.segment_sum(ones, col, num_segments=n_nodes)
        e_agg = sums / jnp.maximum(cnt, 1.0)
        out = jnp.concatenate([x, e_agg, u[batch]], axis=1)
        hid = jax.nn.relu(out @ W1 + b1)
        return hid @ W2 + b2

    def _L2_gnn_ref(feat, weight, src, dst, etypes):
        import jax, jax.numpy as jnp
        import numpy as np
        N_NODES = 6250
        N_EDGES = 100000
        D_IN = 64
        D_OUT = 64
        NUM_RELS = 16
        num_rels = weight.shape[0]
        h_src = feat[src]
        msg = jnp.zeros((h_src.shape[0], weight.shape[2]), dtype=feat.dtype)
        for r in range(num_rels):
            mask = etypes == r
            msg = msg + h_src * mask[:, None].astype(feat.dtype) @ weight[r]
        out = jax.ops.segment_sum(msg, dst, num_segments=feat.shape[0])
        return out

    def _L3_gnn_ref(x, edge_index, edge_attr, u, batch, W1, b1, W2, b2, W3, b3, W4, b4, W5, b5, W6, b6):
        import jax, jax.numpy as jnp
        import numpy as np
        N_NODES = 12500
        N_EDGES = 200000
        N_GRAPHS = 64
        NODE_IN = 64
        EDGE_IN = 32
        GLOBAL_IN = 32
        NODE_OUT = 64
        MSG = 32

        def _linear_params(key, fan_in, fan_out):
            kw, kb = jax.random.split(key)
            s = 1.0 / np.sqrt(fan_in)
            W = jax.random.uniform(kw, (fan_in, fan_out), jnp.float32, -s, s)
            b = jax.random.uniform(kb, (fan_out,), jnp.float32, -s, s)
            return (W, b)
        row, col = (edge_index[0], edge_index[1])
        n = x.shape[0]
        m = jnp.concatenate([x[row], x[col], edge_attr], axis=1)
        h = jnp.maximum(m @ W1 + b1, 0.0)
        h = jnp.maximum(h @ W2 + b2, 0.0)
        h = h @ W3 + b3
        s = jax.ops.segment_sum(h, col, num_segments=n)
        cnt = jax.ops.segment_sum(jnp.ones((h.shape[0], 1), h.dtype), col, num_segments=n)
        agg_mean = s / jnp.maximum(cnt, 1.0)
        agg_max = jax.ops.segment_max(h, col, num_segments=n)
        agg_max = jnp.where(jnp.isfinite(agg_max), agg_max, 0.0)
        o = jnp.concatenate([x, agg_mean, agg_max, u[batch]], axis=1)
        o = jnp.maximum(o @ W4 + b4, 0.0)
        o = jnp.maximum(o @ W5 + b5, 0.0)
        return o @ W6 + b6
    edge_index = jnp.stack([src, dst])
    batch0 = jnp.zeros((12500,), jnp.int32)
    x = _layernorm(x + _L0_gnn_ref(x, edge_attr_64, edge_index, L0_gnn_W1, L0_gnn_b1, L0_gnn_W2, L0_gnn_b2), axis=-1)
    x = _layernorm(x + _L1_gnn_ref(x, edge_attr_16, L1_gnn_u, L1_gnn_W1, L1_gnn_b1, L1_gnn_W2, L1_gnn_b2, edge_index, batch0), axis=-1)
    x = _layernorm(x + _L2_gnn_ref(x, L2_gnn_weight, src, dst, edge_type_16), axis=-1)
    x = _layernorm(x + _L3_gnn_ref(x, edge_index, edge_attr_32, L3_gnn_u, batch0, L3_gnn_W1, L3_gnn_b1, L3_gnn_W2, L3_gnn_b2, L3_gnn_W3, L3_gnn_b3, L3_gnn_W4, L3_gnn_b4, L3_gnn_W5, L3_gnn_b5, L3_gnn_W6, L3_gnn_b6), axis=-1)
    return x

_drawn_inputs = setup_inputs


def setup_inputs(seed=0):
    import zlib

    import numpy as np

    out = dict(_drawn_inputs(seed))
    spreads = {'L0_gnn_b1': (0.0, 2.0),
     'L0_gnn_b2': (0.0, 2.0),
     'L1_gnn_b1': (0.0, 0.8),
     'L1_gnn_b2': (0.0, 0.572)}
    factors = {'edge_attr_32': 8.0,
     'L3_gnn_W1': 8.0,
     'L3_gnn_b1': 33.089,
     'L3_gnn_W2': 8.0,
     'L3_gnn_b2': 62.704,
     'L3_gnn_W3': 7.084,
     'L3_gnn_b3': 182.016,
     'L3_gnn_b4': 140.667,
     'edge_attr_16': 22.757,
     'L3_gnn_u': 22.218,
     'L3_gnn_b5': 8.0,
     'L3_gnn_b6': 7.725,
     'x': 3.864}
    for name, (base, spread) in spreads.items():
        noise = np.random.default_rng([zlib.crc32(name.encode()), seed]).standard_normal(out[name].shape)
        drawn = base * np.exp(spread * noise) if base else spread * noise
        out[name] = jnp.asarray(drawn.astype(out[name].dtype))
    for name, factor in factors.items():
        out[name] = (out[name] * factor).astype(out[name].dtype)
    return out
```

```python
import concourse.bass as bass
from concourse import mybir
from contextlib import ExitStack

F32 = mybir.dt.float32
BF16 = mybir.dt.bfloat16
I32 = mybir.dt.int32
ALU = mybir.AluOpType
ACT = mybir.ActivationFunctionType
AX = mybir.AxisListType

P = 128
N = 12500
E = 400000
T = E // P
NB = -(-N // P)
NP = NB * P
LASTP = N // NB
LASTN = N - LASTP * NB
D = 64
A16, A32 = 16, 32
R1W = D + A16
HID = 128
RELS = 16
MSG = 32
SL = 5
NS = 5
CH = SL * NS
CHUNKS = T // CH
SL3 = 8
NS3 = 4
CH3 = SL3 * NS3
CHUNKS3 = T // CH3
TAIL3 = T - CHUNKS3 * CH3
TAILS3 = [min(SL3, TAIL3 - a) for a in range(0, TAIL3, SL3)]
LANES = 2
NTAB = SL
TABR = NP + P
GB = 7
PAIRS = NB // (2 * GB)
CR, CC = 640, 625
BIG = float(2 ** 20)
HUGE = 3.0e38
EPS = 1e-5


class Steps:

    def __init__(self, eng, sem):
        self.eng, self.sem, self.base, self.n = eng, sem, 0, 0

    def turn(self, base):
        self.base, self.n = base, 0

    def done(self, ins):
        ins.then_inc(self.sem, 1)
        self.n += 1
        return self.n

    def wait(self, n):
        self.eng.wait_ge(self.sem, self.base + n)

    def link(self, ins):
        self.wait(self.done(ins))


def is_first(c):
    return isinstance(c, int) and c == 0


def turns(eng, n, body, steps=None, per=0):
    body(0)
    assert steps is None or steps.n == per, (steps.n, per)
    with eng.Fori(1, n) as c:
        body(c)


def hold(eng, sem, n, passed):
    eng.wait_ge(sem, n)
    if not isinstance(n, int):
        eng.sem_inc(passed, 1)


def copy_at(v, out, in_):
    return v.tensor_scalar(out, in_, 1.0, None, ALU.mult)


def gather(eng, out, table, index, sem):
    eng.indirect_dma_start(out=out, out_offset=None, in_=table,
                           in_offset=bass.IndirectOffsetOnAxis(ap=index, axis=0)).then_inc(sem, 16)


def scatter(eng, table, index, in_, sem, add=False):
    kw = {"compute_op": ALU.add} if add else {}
    eng.indirect_dma_start(out=table, out_offset=bass.IndirectOffsetOnAxis(ap=index, axis=0),
                           in_=in_, in_offset=None, **kw).then_inc(sem, 16)


def over(ap, axis, n):
    return ap.unsqueeze(axis).to_broadcast([*ap.shape[:axis], n, *ap.shape[axis:]])


class Kernel:
    pass


def setup(nc, k, ins):
    with ExitStack() as ctx:
        def sb(name, shape, dt=F32):
            return ctx.enter_context(nc.sbuf_tensor(name, shape, dt))

        def sem(name):
            return ctx.enter_context(nc.semaphore(name))

        dst_i = sb("dst_i", [P, T], I32)
        src_i = sb("src_raw", [P, T], I32)
        typ_i = sb("typ_i", [P, T], I32)
        dst_f = sb("dst_f", [P, T])
        coarse5 = sb("coarse5", [P, CR // P], I32)
        coarse5f = sb("coarse5f", [P, CR // P])
        coarse = sb("coarse", [P, CR])
        junk = sb("junk", [P, CR])
        rows = sb("rows", [P, GB, CC], I32)
        nid_i = sb("nid_i", [P, NB], I32)
        ncol = sb("ncol", [P, 2, GB])
        rcount = sb("rcount", [P, 2, GB])
        rfound = sb("rfound", [P, 2, GB])
        row_i = sb("row_i", [P, 2, GB], I32)
        end_f = sb("end_f", [P, NB])
        end_i = sb("end_i", [P, NB], I32)
        start_i = sb("start_i", [P, NB], I32)
        start_f = sb("start_f", [P, NB])
        cnt = sb("cnt", [P, NB])
        tmp = sb("tmp", [P, NB])
        pid_i = sb("pid_i", [P, 1], I32)
        pid = sb("pid", [P, 1])
        fend_i = sb("fend_i", [P, 1], I32)
        fidx = sb("fidx", [P, 1], I32)
        fend = sb("fend", [P, 1])
        cols = sb("cols", [P, 4])
        bigsel = sb("bigsel", [P, P])
        lastr = sb("lastr", [MSG, P])
        firstr = sb("firstr", [MSG, P])
        one_i = sb("one_i", [1, 1], I32)
        l_idx, l_x, l_w, l_c5, l_co = (sem(s) for s in ("l_idx", "l_x", "l_w", "l_c5", "l_co"))
        consts, wzero = sem("consts"), sem("wzero")
        c5_ready, c5_saved, row_ready = sem("c5_ready"), sem("c5_saved"), sem("row_ready")
        row_got = [sem(f"row_got{r}") for r in range(GB)]
        row_used = sem("row_used")
        end_ready, end_saved, start_got = sem("end_ready"), sem("end_saved"), sem("start_got")
        zero_put, fend_got, one_ready = sem("zero_put"), sem("fend_got"), sem("one_ready")
        steps, rows_built, search = sem("setup_steps"), sem("rows_built"), sem("search_steps")
        psS = k.ps[:, 0, 0:P]
        psL = k.ps[0:MSG, 1, 0:P]
        psF = k.ps[0:MSG, 2, 0:P]
        nodes = k.X[0:LASTP, :, :]
        NW = len(k.loads)

        block = ctx.enter_context(nc.Block())

        @block.sync
        def _(sp):
            sp.dma_start(coarse5[:, :], ins["dst"].rearrange("(p j c) -> p j c", p=P, c=CC)[:, :, 0],
                         allow_slow_non_contiguous=True).then_inc(l_c5, 16)
            sp.dma_start(dst_i[:, :], ins["dst"].rearrange("(p t) -> p t", p=P)).then_inc(l_idx, 16)
            sp.dma_start(src_i[:, :], ins["src"].rearrange("(p t) -> p t", p=P)).then_inc(l_idx, 16)
            sp.dma_start(typ_i[:, :], ins["edge_type_16"].rearrange("(p t) -> p t", p=P)).then_inc(l_idx, 16)
            sp.wait_ge(wzero, 6)
            sp.dma_start(nodes, ins["x"][0:LASTP * NB, :].rearrange("(p b) f -> p b f", b=NB)).then_inc(l_x, 16)
            sp.dma_start(k.X[LASTP:LASTP + 1, 0:LASTN, :],
                         ins["x"][LASTP * NB:N, :].rearrange("(p b) f -> p b f", p=1)).then_inc(l_x, 16)
            for dst, src in k.loads:
                sp.dma_start(dst, src, allow_slow_non_contiguous=True).then_inc(l_w, 16)
            sp.wait_ge(c5_ready, 1)
            sp.dma_start(k.coarse_d.rearrange("(p j) -> p j", p=P), coarse5f[:, :]).then_inc(c5_saved, 16)
            sp.wait_ge(c5_saved, 16)
            sp.dma_start(coarse[:, :], k.coarse_d.rearrange("(a n) -> a n", a=1).to_broadcast([P, CR])).then_inc(l_co, 16)
            for tab in k.tables:
                flat = tab.rearrange("(p a) f -> p (a f)", p=P)
                w = TABR * D // P
                for q in range(4):
                    sp.dma_start(flat[:, q * w // 4:(q + 1) * w // 4], k.zeros[:, 0:w // 4]).then_inc(zero_put, 16)
            for r, w in ((k.R1, R1W), (k.R2, D), (k.R3, D)):
                sp.dma_start(r[E:E + P, :], k.zeros[:, 0:w]).then_inc(zero_put, 16)
            sp.wait_ge(one_ready, 1)
            sp.dma_start(k.ends[0:1, :], one_i[:, :]).then_inc(end_saved, 16)
            sp.wait_ge(end_ready, 1)
            sp.dma_start(k.ends[1:NP + 1, :].rearrange("(p b) a -> p (b a)", b=NB), end_i[:, :]).then_inc(end_saved, 16)
            sp.wait_ge(end_saved, 32)
            sp.dma_start(start_i[:, :], k.ends[0:NP, :].rearrange("(p b) a -> p (b a)", b=NB)).then_inc(start_got, 16)
            sp.wait_ge(l_x, 32)
            sp.wait_ge(l_w, 16 * NW)
            sp.wait_ge(zero_put, 16 * (4 * NTAB + 3))

        @block.gpsimd
        def _(pool):
            pool.memset(k.ident[:, :], 0.0).then_inc(consts, 1)
            pool.memset(k.upper[:, :, :], 0.0).then_inc(consts, 1)
            pool.memset(bigsel[:, :], 0.0).then_inc(consts, 1)
            pool.wait_ge(consts, 3)
            pool.affine_select(out=k.ident[:, :], in_=k.ident[:, :], compare_op=ALU.not_equal, fill=1.0,
                               base=0, pattern=[[-1, P]], channel_multiplier=1).then_inc(consts, 1)
            pool.affine_select(out=k.upper[:, :, :], in_=k.upper[:, :, :], compare_op=ALU.is_ge, fill=BIG,
                               base=0, pattern=[[0, 4], [1, P]], channel_multiplier=-1).then_inc(consts, 1)
            pool.affine_select(out=bigsel[:, :], in_=bigsel[:, :], compare_op=ALU.is_ge, fill=BIG,
                               base=-1, pattern=[[1, P]], channel_multiplier=-1).then_inc(consts, 1)
            pool.iota(nid_i[:, :], pattern=[[1, NB]], base=0, channel_multiplier=NB).then_inc(consts, 1)
            pool.iota(pid_i[:, :], pattern=[[1, 1]], base=0, channel_multiplier=1).then_inc(consts, 1)
            pool.memset(one_i[:, :], 0).then_inc(one_ready, 1)
            def body(c):
                for q in range(2):
                    hold(pool, row_ready, 2 * c + q + 1, k.passed)
                    for b in range(GB):
                        if not (is_first(c) and q == 0):
                            hold(pool, row_used, GB * (2 * c + q - 1) + b + 1, k.passed)
                        gather(pool, rows[:, b, :], ins["dst"].rearrange("(r c) -> r c", c=CC),
                               row_i[:, q, b:b + 1], row_got[b])

            turns(pool, PAIRS, body)
            pool.wait_ge(end_saved, 32)
            gather(pool, fend_i[:, :], k.ends, fidx[:, :], fend_got)

        @block.tensor
        def _(pe):
            pe.wait_ge(consts, 8)
            pe.wait_ge(steps, 8)
            nc.tensor.matmul(psS, cols[:, 0:1].to_broadcast([P, P]), k.ident[:, :], start=True, stop=False)
            nc.tensor.matmul(psS, k.ident[:, :], bigsel[:, :], start=False, stop=True)
            nc.tensor.matmul(psL, cols[:, 1:2].to_broadcast([P, MSG]), k.ident[:, :], start=True, stop=True)
            nc.tensor.matmul(psF, cols[:, 0:1].to_broadcast([P, MSG]), k.ident[:, :], start=True, stop=True)\
                .then_inc(rows_built, 1)

        @block.vector
        def _(v):
            s = Steps(v, steps)
            v.memset(k.zeros[:, :], 0.0).then_inc(wzero, 1)
            v.memset(k.W1e[:, :], 0.0).then_inc(wzero, 1)
            v.memset(k.W2e[:, :], 0.0).then_inc(wzero, 1)
            v.memset(k.W3e[:, :], 0.0).then_inc(wzero, 1)
            v.memset(k.X[96:P, LASTN:NB, :], 0.0).then_inc(wzero, 1)
            v.memset(k.b1z[:, :], 0.0).then_inc(wzero, 1)
            v.memset(k.ones[:, :], 1.0)
            v.wait_ge(l_c5, 16)
            v.tensor_copy(coarse5f[:, :], coarse5[:, :]).then_inc(c5_ready, 1)
            v.wait_ge(l_idx, 48)
            s.done(v.tensor_copy(dst_f[:, :], dst_i[:, :]))
            s.done(v.tensor_copy(k.src[:, 0:T], src_i[:, :]))
            s.done(v.memset(k.src[:, T:], 0.0))
            s.done(v.memset(k.same[:, T:], 0.0))
            s.done(v.memset(k.same[:, 0:1], 0.0))
            s.wait(1)
            s.done(v.tensor_tensor(k.same[:, 1:T], dst_f[:, 1:T], dst_f[:, 0:T - 1], ALU.is_equal))
            s.done(v.tensor_copy(cols[:, 0:1], dst_f[:, 0:1]))
            s.done(v.tensor_copy(cols[:, 1:2], dst_f[:, T - 1:T]))
            assert s.n == 8
            s.done(v.tensor_copy(k.firstf[:, :], dst_f[:, 0:1]))
            s.wait(s.n)
            s.done(v.scalar_tensor_tensor(out=k.rel_i[:, :], in0=k.src[:, 0:T], scalar=float(RELS), in1=typ_i[:, :],
                                   op0=ALU.mult, op1=ALU.add))
            v.wait_ge(consts, 8)
            s.done(v.tensor_copy(k.nid[:, :], nid_i[:, :]))
            s.done(v.tensor_copy(pid[:, :], pid_i[:, :]))
            s.wait(s.n)
            s.done(v.tensor_scalar(k.dump[:, 0:T], k.src[:, 0:T], -1.0, float(NP), ALU.mult, ALU.add))
            s.wait(s.n)
            s.link(v.tensor_scalar(k.dump[:, 0:T], k.dump[:, 0:T], pid[:, 0:1], None, ALU.add))
            s.done(v.memset(k.dump[:, T:], 0.0))
            v.wait_ge(l_co, 16)
            s.wait(s.n)
            f = Steps(v, search)
            def body(c):
                f.turn(PER * c)
                for q in range(2):
                    f.link(copy_at(v, ncol[:, q], k.nid[:, bass.ds((2 * c + q) * GB, GB)]))
                    for b in range(GB):
                        f.link(v.tensor_scalar(junk[:, 0:CR], coarse[:, :], ncol[:, q, b:b + 1], 0.0, ALU.is_le,
                                               ALU.add, accum_out=rcount[:, q, b:b + 1]))
                    f.link(v.tensor_scalar(rcount[:, q], rcount[:, q], -1.0, 0.0, ALU.add, ALU.max))
                    v.tensor_copy(row_i[:, q], rcount[:, q]).then_inc(row_ready, 1)
                for q in range(2):
                    for b in range(GB):
                        v.wait_ge(row_got[b], 16 * (2 * c + q + 1))
                        v.tensor_scalar(junk[:, 0:CC], rows[:, b, :], ncol[:, q, b:b + 1], 0.0, ALU.is_le,
                                        ALU.add, accum_out=rfound[:, q, b:b + 1]).then_inc(row_used, 1)
                        v.wait_ge(row_used, GB * (2 * c + q) + b + 1)
                    f.link(v.scalar_tensor_tensor(out=end_f[:, bass.ds((2 * c + q) * GB, GB)], in0=rcount[:, q],
                                                  scalar=float(CC), in1=rfound[:, q], op0=ALU.mult, op1=ALU.add))

            PER = 2 * (GB + 3)
            turns(v, PAIRS, body, f, PER)
            s.done(v.tensor_scalar(fidx[:, :], cols[:, 0:1], 1.0, None, ALU.add))
            v.tensor_copy(end_i[:, :], end_f[:, :]).then_inc(end_ready, 1)
            s.link(v.tensor_scalar(tmp[:, :], end_f[:, :], -1.0, 0.0, ALU.add, ALU.max))
            s.done(v.tensor_copy(k.last_i[:, :], tmp[:, :]))
            v.wait_ge(start_got, 16)
            s.link(v.tensor_copy(start_f[:, :], start_i[:, :]))
            s.link(v.tensor_tensor(cnt[:, :], end_f[:, :], start_f[:, :], ALU.subtract))
            s.done(v.tensor_scalar(k.some[:, :], cnt[:, :], 0.5, None, ALU.is_gt))
            s.link(v.tensor_scalar(cnt[:, :], cnt[:, :], 1.0, None, ALU.max))
            s.link(v.reciprocal(k.rcnt[:, :], cnt[:, :]))
            s.link(v.tensor_scalar(cnt[:, :], k.nid[:, :], float(E), None, ALU.add))
            s.link(v.tensor_tensor(start_f[:, :], start_f[:, :], cnt[:, :], ALU.subtract))
            s.link(v.tensor_tensor(start_f[:, :], start_f[:, :], k.some[:, :], ALU.mult))
            s.link(v.tensor_tensor(cnt[:, :], start_f[:, :], cnt[:, :], ALU.add))
            s.done(v.tensor_copy(k.zrow_i[:, :], cnt[:, :]))
            v.wait_ge(fend_got, 16)
            s.link(v.tensor_copy(fend[:, :], fend_i[:, :]))
            s.link(v.tensor_scalar(cols[:, 2:3], pid[:, :], float(T), float(T), ALU.mult, ALU.add))
            s.link(v.tensor_tensor(cols[:, 2:3], fend[:, :], cols[:, 2:3], ALU.is_le))
            s.link(v.tensor_scalar(cols[:, 3:4], pid[:, :], float(E), None, ALU.add))
            s.link(v.tensor_scalar(fend[:, :], fend[:, :], -1.0, cols[:, 3:4], ALU.add, ALU.subtract))
            s.link(v.scalar_tensor_tensor(out=fend[:, :], in0=fend[:, :], scalar=cols[:, 2:3], in1=cols[:, 3:4],
                                          op0=ALU.mult, op1=ALU.add))
            s.done(v.tensor_copy(k.fix_i[:, :], fend[:, :]))
            v.wait_ge(rows_built, 1)
            s.done(v.tensor_scalar(k.before[:, :], psS, cols[:, 1:2], None, ALU.is_equal))
            s.link(v.tensor_copy(lastr[:, :], psL))
            s.link(v.tensor_copy(firstr[:, :], psF))
            for out, a in ((k.chain, lastr), (k.joins, firstr)):
                s.link(v.tensor_tensor(out[:, 1:P], a[:, 1:P], lastr[:, 0:P - 1], ALU.is_equal))
                s.link(v.memset(out[:, 0:1], 0.0))
                s.link(v.tensor_scalar(out[:, :], out[:, :], 1.0, HUGE, ALU.subtract, ALU.mult))


def edges_01(nc, k, ins):
    with ExitStack() as ctx:
        def sb(name, shape, dt=F32):
            return ctx.enter_context(nc.sbuf_tensor(name, shape, dt))

        def sem(name):
            return ctx.enter_context(nc.semaphore(name))

        v64 = sb("v64", [P, NS, SL, D])
        v16 = sb("v16", [P, NS, SL, A16])
        run = sb("run", [P, NS, SL, R1W])
        meta = sb("meta", [P, NS, 3, SL])
        mates = sb("mates", [P, 3, SL, P])
        later = sb("later", [P, 2, SL])
        route = sb("route", [P, 2, SL])
        row_i = sb("row_i1", [P, NS, SL], I32)
        sums = sb("sums", [P, NS, SL, D])
        loaded = [sem(f"loaded{q}") for q in range(NS)]
        stored = [sem(f"stored{q}") for q in range(NS)]
        added = [sem(f"added{q}") for q in range(NTAB)]
        meta_ready, spread, mates_ready, row_ready, run_ready, summed, sums_ready, vsteps = (
            sem(s) for s in ("meta_ready", "spread", "mates_ready", "row_ready1", "run_ready", "summed",
                             "sums_ready", "vsteps1"))
        e64 = ins["edge_attr_64"].rearrange("(p t) f -> p t f", p=P)
        e16 = ins["edge_attr_16"].rearrange("(p t) f -> p t f", p=P)
        R1 = k.R1[0:E, :].rearrange("(p t) f -> p t f", p=P)
        SLOTS = CHUNKS * NS

        def ps_spread(q):
            return k.psf[:, (q % 3) * 1024:(q % 3) * 1024 + SL * P]

        def ps_sum(q):
            return k.ps[:, 6 + q % 2, 0:SL * D]

        block = ctx.enter_context(nc.Block())

        @block.sync
        def _(sp):
            def load(c, q):
                at = c * CH + q * SL
                sp.dma_start(v64[:, q], e64[:, bass.ds(at, SL), :]).then_inc(loaded[q], 16)
                sp.dma_start(v16[:, q], e16[:, bass.ds(at, SL), :]).then_inc(loaded[q], 16)

            def store(c, q):
                sp.wait_ge(run_ready, NS * c + q + 1)
                sp.dma_start(R1[:, bass.ds(c * CH + q * SL, SL), :], run[:, q]).then_inc(stored[q], 16)

            for q in range(NS):
                load(0, q)
            with sp.Fori(0, CHUNKS - 1) as c:
                for q in range(NS):
                    store(c, q)
                    sp.wait_ge(summed, NS * c + q + 1)
                    load(c + 1, q)
            for q in range(NS):
                store(CHUNKS - 1, q)
            for q in range(NS):
                sp.wait_ge(stored[q], 16 * CHUNKS)

        @block.scalar
        def _(act):
            def copy_meta(c, q, at_first):
                if not at_first:
                    act.wait_ge(run_ready, NS * c + q + 1 - NS)
                    act.wait_ge(row_ready, NS * c + q + 1 - NS)
                at = c * CH + q * SL
                for j, a in enumerate((k.src, k.same, k.dump)):
                    last = act.copy(meta[:, q, j, :], a[:, bass.ds(at, SL)])
                    last.then_inc(meta_ready, 1)

            def body(c):
                for q in range(NS):
                    n = NS * c + q
                    copy_meta(c + (q + 1) // NS, (q + 1) % NS, is_first(c) and q < NS - 1)
                    act.wait_ge(summed, n + 1)
                    if not is_first(c):
                        act.wait_ge(added[NTAB - 1], 16 * (n - NS + 2))
                    act.copy(sums[:, q].rearrange("p t f -> p (t f)"), ps_sum(q)).then_inc(sums_ready, 1)

            copy_meta(0, 0, True)
            turns(act, CHUNKS, body)

        @block.tensor
        def _(pe):
            def spread_src(c, q, n, at_first):
                pe.wait_ge(meta_ready, 3 * n + 3)
                if not at_first:
                    pe.wait_ge(mates_ready, n - 1)
                ps = ps_spread(q)
                for t in range(SL):
                    nc.tensor.matmul(ps[:, t * P:(t + 1) * P], meta[:, q, 0, t:t + 1].to_broadcast([P, P]),
                                     k.ident[:, :], start=t in (0, 4), stop=False)
                nc.tensor.matmul(ps[:, 0:4 * P], k.ident[:, :],
                                 k.upper[:, :, :].rearrange("p a i -> p (a i)"), start=False, stop=True)
                nc.tensor.matmul(ps[:, 4 * P:5 * P], k.ident[:, :], k.upper[:, 0, :],
                                 start=False, stop=True).then_inc(spread, 1)

            def body(c):
                for q in range(NS):
                    n = NS * c + q
                    spread_src(c + (q + 1) // NS, (q + 1) % NS, n + 1, is_first(c) and q < 1)
                    pe.wait_ge(mates_ready, n + 1)
                    pe.wait_ge(loaded[q], 32 * c + 32)
                    if not (is_first(c) and q < 2):
                        pe.wait_ge(sums_ready, n - 1 if q else n)
                    for t in range(SL):
                        last = nc.tensor.matmul(ps_sum(q)[:, t * D:(t + 1) * D], mates[:, q % 3, t, :],
                                                v64[:, q, t, :], start=True, stop=True)
                    last.then_inc(summed, 1)

            spread_src(0, 0, 0, True)
            turns(pe, CHUNKS, body)

        @block.vector
        def _(v):
            s = Steps(v, vsteps)
            s.link(v.memset(run[:, NS - 1, SL - 1, :], 0.0))

            def body(c):
                s.turn(1 + PER * c)
                for q in range(NS):
                    n = NS * c + q
                    before = (q - 1) % NS

                    def sum_step(t):
                        p64 = run[:, q, t - 1, 0:D] if t else run[:, before, SL - 1, 0:D]
                        p16 = run[:, q, t - 1, D:] if t else run[:, before, SL - 1, D:]
                        s.done(v.scalar_tensor_tensor(out=run[:, q, t, 0:D], in0=p64, scalar=meta[:, q, 1, t:t + 1],
                                                      in1=v64[:, q, t, :], op0=ALU.mult, op1=ALU.add))
                        ins_ = v.scalar_tensor_tensor(out=run[:, q, t, D:], in0=p16, scalar=meta[:, q, 1, t:t + 1],
                                                      in1=v16[:, q, t, :], op0=ALU.mult, op1=ALU.add)
                        if t == SL - 1:
                            ins_.then_inc(run_ready, 1)
                            return None
                        return s.done(ins_)

                    v.wait_ge(spread, n + 1)
                    if not (is_first(c) and q < 2):
                        v.wait_ge(summed, n - 1)
                    v.tensor_tensor(mates[:, q % 3], ps_spread(q).rearrange("p (t i) -> p t i", t=SL),
                                    over(meta[:, q, 0, :], 2, P), ALU.is_equal).then_inc(mates_ready, 1)
                    v.wait_ge(loaded[q], 32 * c + 32)
                    if not is_first(c):
                        v.wait_ge(stored[q], 16 * c)
                    if q or not is_first(c):
                        v.wait_ge(run_ready, n)
                    prev = sum_step(0)
                    v.wait_ge(mates_ready, n + 1)
                    m1 = s.done(v.tensor_reduce(later[:, q % 2, :], mates[:, q % 3], AX.X, ALU.add))
                    s.wait(prev)
                    prev = sum_step(1)
                    s.wait(m1)
                    m2 = s.done(v.scalar_tensor_tensor(out=route[:, q % 2, :], in0=later[:, q % 2, :], scalar=1.5,
                                                       in1=meta[:, q, 2, :], op0=ALU.is_gt, op1=ALU.mult))
                    s.wait(prev)
                    prev = sum_step(2)
                    s.wait(m2)
                    if not is_first(c):
                        v.wait_ge(added[NTAB - 1], 16 * (n - NS + 2))
                    v.tensor_tensor(row_i[:, q, :], route[:, q % 2, :], meta[:, q, 0, :], ALU.add).then_inc(row_ready, 1)
                    for t in range(3, SL):
                        s.wait(prev)
                        prev = sum_step(t)

            PER = NS * (2 * SL + 1)
            turns(v, CHUNKS, body, s, PER)
            v.wait_ge(run_ready, SLOTS)
            v.tensor_copy(k.tail[:, :], run[:, NS - 1, SL - 1, :])

        @block.gpsimd
        def _(pool):
            def body(c):
                for q in range(NS):
                    n = NS * c + q
                    hold(pool, sums_ready, n + 1, k.passed)
                    hold(pool, row_ready, n + 1, k.passed)
                    for t in range(SL):
                        if not (is_first(c) and q == 0):
                            hold(pool, added[t], 16 * n, k.passed)
                        scatter(pool, k.tables[t], row_i[:, q, t:t + 1], sums[:, q, t, :], added[t], add=True)

            turns(pool, CHUNKS, body)
            for t in range(SL):
                pool.wait_ge(added[t], 16 * SLOTS)

    fix_rows(nc, k, 1, k.R1, R1W, False)


def fix_rows(nc, k, n, rows, width, maxima):
    with ExitStack() as ctx:
        def sb(name, shape, dt=F32):
            return ctx.enter_context(nc.sbuf_tensor(name, shape, dt))

        g = sb(f"fix_rows{n}", [P, width])
        lastT, runT, carT = (sb(f"{s}{n}", [MSG, P]) for s in ("fix_last", "fix_run", "fix_carry"))
        got, put, pe_steps, v_steps = (ctx.enter_context(nc.semaphore(f"{s}{n}"))
                                       for s in ("fix_got", "fix_put", "fix_pe", "fix_v"))
        sums = width // 2 if maxima else width
        psS, psT, psM = k.ps[:, 0, 0:sums], k.ps[0:MSG, 1, 0:P], k.ps[:, 2, 0:MSG]
        ready = 6 if maxima else 1

        block = ctx.enter_context(nc.Block())

        @block.gpsimd
        def _(pool):
            gather(pool, g[:, :], rows, k.fix_i[:, :], got)
            pool.wait_ge(v_steps, ready)
            scatter(pool, rows, k.fix_i[:, :], g[:, :], put)
            pool.wait_ge(put, 16)

        @block.tensor
        def _(pe):
            nc.tensor.matmul(psS, k.before[:, :], k.tail[:, 0:sums], start=True, stop=True).then_inc(pe_steps, 1)
            if maxima:
                nc.tensor.transpose(psT, k.tail[:, sums:width], k.ident[:, :]).then_inc(pe_steps, 1)
                pe.wait_ge(v_steps, 5)
                nc.tensor.transpose(psM, carT[:, :], k.ident[0:MSG, 0:MSG]).then_inc(pe_steps, 1)

        @block.vector
        def _(v):
            s = Steps(v, v_steps)
            v.wait_ge(got, 16)
            v.wait_ge(pe_steps, 1)
            s.link(v.tensor_tensor(g[:, 0:sums], g[:, 0:sums], psS, ALU.add))
            if maxima:
                v.wait_ge(pe_steps, 2)
                s.link(v.tensor_copy(lastT[:, :], psT))
                s.link(v.tensor_tensor_scan(out=runT[:, :], data0=k.chain[:, :], data1=lastT[:, :], initial=0.0,
                                            op0=ALU.add, op1=ALU.max))
                s.link(v.memset(carT[:, 0:1], -HUGE))
                s.link(v.tensor_tensor(carT[:, 1:P], runT[:, 0:P - 1], k.joins[:, 1:P], ALU.add))
                v.wait_ge(pe_steps, 3)
                s.done(v.tensor_tensor(g[:, sums:], g[:, sums:], psM, ALU.max))


def norm(v, s, y, x_out, st, sq, std_in, std, eng_wait, act_sem, done=None):
    s.link(v.tensor_reduce(st[:, 0, :], y, AX.X, ALU.add))
    s.link(v.tensor_scalar(st[:, 0, :], st[:, 0, :], 1.0 / D, None, ALU.mult))
    s.link(v.tensor_tensor(y, y, over(st[:, 0, :], 2, D), ALU.subtract))
    s.link(v.tensor_tensor(sq, y, y, ALU.mult))
    s.link(v.tensor_reduce(st[:, 1, :], sq, AX.X, ALU.add))
    v.tensor_scalar(std_in, st[:, 1, :], 1.0 / D, EPS, ALU.mult, ALU.add).then_inc(act_sem, 1)
    eng_wait()
    s.link(v.reciprocal(st[:, 2, :], std))
    last = v.tensor_tensor(x_out, y, over(st[:, 2, :], 2, D), ALU.mult)
    if done is None:
        s.link(last)
    else:
        last.then_inc(done, 1)


def nodes_01(nc, k, ins):
    with ExitStack() as ctx:
        def sb(name, shape, dt=F32):
            return ctx.enter_context(nc.sbuf_tensor(name, shape, dt))

        def sem(name):
            return ctx.enter_context(nc.semaphore(name))

        tabs = sb("tabs", [P, 2, NTAB, GB * D])
        got = sb("got", [P, 2, GB, R1W])
        idx = sb("idx", [P, 2, GB], I32)
        cat = sb("cat", [P, 2, GB, HID])
        cat1 = sb("cat1", [P, 2, GB, R1W])
        catT = sb("catT", [P, GB * P])
        hT = sb("hT", [P, GB * P])
        y = sb("y", [P, GB, D])
        sq = sb("sq", [P, GB, D])
        st = sb("st", [P, 3, GB])
        std_in = sb("std_in", [P, GB])
        std = sb("std", [P, GB])
        x2 = sb("x2", [P, GB, D])
        x2T = sb("x2T", [D, GB * P])
        tab = sb("tab", [P, 2, RELS * D])
        ub = sb("ub", [P, 1])
        tabs_got = [sem(f"tabs_got{q}") for q in range(2)]
        rows_got = [sem(f"rows_got{q}") for q in range(2)]
        tab_put = [sem(f"tab_put{q}") for q in range(2)]
        idx_ready, agg_done, cat_ready, turned, turned_c, hid, hid_r, outp, vsteps, var, root, rows2, tab_ready, tab_ready_v, ubs, x_in = (
            sem(s) for s in ("idx_ready", "agg_done", "cat_ready", "turned", "turned_c", "hid", "hid_r", "outp",
                             "nsteps", "var", "root", "rows2", "tab_ready", "tab_ready_v", "ubs", "x_in"))
        Y = k.Y.rearrange("(p b r) f -> p b (r f)", p=P, b=NB)
        psT, psH, psY = k.psf[:, 0:GB * P], k.psf[:, 1024:1024 + GB * P], k.ps[:, 4, 0:GB * D]
        psR = [k.psf[:, 3072:4096], k.psf[:, 1024:2048]]
        halves = ((0, 512), (512, GB * P))

        block = ctx.enter_context(nc.Block())

        @block.sync
        def _(sp):
            def body(c):
                for q in range(2):
                    g = 2 * c + q
                    if not is_first(c):
                        sp.wait_ge(agg_done, g - 1)
                    for t in range(NTAB):
                        sp.dma_start(tabs[:, q, t, :],
                                     k.tables[t][0:NP, :].rearrange("(p b) f -> p (b f)", p=P)
                                     [:, bass.ds(g * GB * D, GB * D)]).then_inc(tabs_got[q], 16)
                for q in range(2):
                    for b in range(GB):
                        n = (2 * c + q) * GB + b
                        sp.wait_ge(tab_ready, n + 1)
                        sp.wait_ge(tab_ready_v, n + 1)
                        sp.dma_start(Y[:, bass.ds((2 * c + q) * GB + b, 1), :], tab[:, (q * GB + b) % 2, None, :]).then_inc(tab_put[(q * GB + b) % 2], 16)

            turns(sp, PAIRS, body)
            for q in range(2):
                sp.wait_ge(tab_put[q], 16 * PAIRS * GB)

        @block.gpsimd
        def _(pool):
            def body(c):
                for q in range(2):
                    hold(pool, idx_ready, 2 * c + q + 1, k.passed)
                    for b in range(GB):
                        gather(pool, got[:, q, b, :], k.R1, idx[:, q, b:b + 1], rows_got[q])

            turns(pool, PAIRS, body)

        @block.tensor
        def _(pe):
            nc.tensor.matmul(k.ps[:, 5, 0:1], k.W1bu[:, :], k.u1[:, :], start=True, stop=True).then_inc(ubs, 1)

            def mlp(step, src, w, W1, W2, b2):
                pe.wait_ge(cat_ready, step + 1)
                for b in range(GB):
                    last = nc.tensor.transpose(psT[0:w, b * P:(b + 1) * P], src[:, b, :], k.ident[:, :])
                last.then_inc(turned, 1)
                for a, z in halves:
                    pe.wait_ge(turned_c, 2 * step + 2)
                    last = nc.tensor.matmul(psH[:, a:z], W1, catT[0:w, a:z], start=True, stop=True)
                last.then_inc(hid, 1)
                nc.tensor.matmul(psY, k.ones[0:1, :], over(b2, 1, GB), start=True, stop=False)
                pe.wait_ge(hid_r, 2 * step + 2)
                for b in range(GB):
                    last = nc.tensor.matmul(psY[:, b * D:(b + 1) * D], hT[:, b * P:(b + 1) * P], W2,
                                            start=False, stop=b == GB - 1)
                last.then_inc(outp, 1)

            def body(c):
                for q in range(2):
                    g = 2 * c + q
                    mlp(2 * g, cat[:, q], HID, k.W1a[:, :], k.W2a[:, :], k.b2a[0:1, :])
                    mlp(2 * g + 1, cat1[:, q], R1W, k.W1b[:, :], k.W2b[:, :], k.b2b[0:1, :])
                    hold(pe, rows2, 2 * g + 1, k.passed)
                    for b in range(GB):
                        last = nc.tensor.transpose(psT[0:D, b * P:(b + 1) * P], x2[:, b, :], k.ident[:, :])
                    last.then_inc(turned, 1)
                    pe.wait_ge(rows2, 2 * g + 2)
                    for b in range(GB):
                        n = g * GB + b
                        if not (is_first(c) and q == 0 and b < 2):
                            pe.wait_ge(tab_ready, n - 1)
                            pe.wait_ge(tab_ready_v, n - 1)
                        for h in range(2):
                            last = nc.tensor.matmul(psR[b % 2][:, h * 512:(h + 1) * 512], x2T[:, b * P:(b + 1) * P],
                                                    k.W2r[:, :, :].rearrange("i r o -> i (r o)")[:, h * 512:(h + 1) * 512],
                                                    start=True, stop=True)
                        last.then_inc(ubs, 1)
                    pe.wait_ge(tab_ready, (g + 1) * GB)
                    pe.wait_ge(tab_ready_v, (g + 1) * GB)

            turns(pe, PAIRS, body)

        @block.scalar
        def _(act):
            ones = [0]

            def relu(step, bias):
                act.wait_ge(hid, step + 1)
                for a, z in halves:
                    act.activation(hT[:, a:z], psH[:, a:z], ACT.Relu, bias=bias).then_inc(hid_r, 1)

            def body(c):
                for q in range(2):
                    g = 2 * c + q
                    act.wait_ge(turned, 3 * g + 1)
                    act.copy(catT[:, 0:512], psT[:, 0:512]).then_inc(turned_c, 1)
                    act.copy(catT[:, 512:], psT[:, 512:]).then_inc(turned_c, 1)
                    relu(2 * g, k.b1a[:, 0:1])
                    act.wait_ge(var, 2 * g + 1)
                    act.activation(std[:, :], std_in[:, :], ACT.Sqrt).then_inc(root, 1)
                    act.wait_ge(turned, 3 * g + 2)
                    act.copy(catT[0:R1W, 0:512], psT[0:R1W, 0:512]).then_inc(turned_c, 1)
                    act.copy(catT[0:R1W, 512:], psT[0:R1W, 512:]).then_inc(turned_c, 1)
                    relu(2 * g + 1, ub[:, 0:1])
                    act.wait_ge(var, 2 * g + 2)
                    act.activation(std[:, :], std_in[:, :], ACT.Sqrt).then_inc(root, 1)
                    act.wait_ge(turned, 3 * g + 3)
                    act.copy(x2T[:, :], psT[0:D, :]).then_inc(rows2, 1)
                    for b in range(GB):
                        n = g * GB + b
                        act.wait_ge(ubs, n + 2)
                        if not (is_first(c) and q * GB + b < 2):
                            act.wait_ge(tab_put[(q * GB + b) % 2], 16 * (GB * c + (q * GB + b) // 2))
                        act.copy(tab[:, (q * GB + b) % 2, 0:512], psR[b % 2][:, 0:512]).then_inc(tab_ready, 1)

            act.wait_ge(ubs, 1)
            act.activation(ub[:, :], k.ps[:, 5, 0:1], ACT.Identity, bias=k.b1b[:, 0:1]).then_inc(x_in, 1)
            act.wait_ge(x_in, 1)
            turns(act, PAIRS, body)

        @block.vector
        def _(v):
            s = Steps(v, vsteps)

            def body(c):
                s.turn(PER * c)
                for q in range(2):
                    g = 2 * c + q
                    blk = bass.ds(g * GB, GB)
                    if not is_first(c):
                        v.wait_ge(agg_done, g - 1)
                    copy_at(v, idx[:, q], k.last_i[:, blk]).then_inc(idx_ready, 1)
                for q in range(2):
                    g = 2 * c + q
                    blk = bass.ds(g * GB, GB)
                    v.wait_ge(tabs_got[q], 16 * NTAB * (c + 1))
                    v.wait_ge(rows_got[q], 16 * GB * (c + 1))
                    agg = cat[:, q, :, D:]
                    s.link(v.tensor_tensor(cat1[:, q], got[:, q], over(k.some[:, blk], 2, R1W), ALU.mult))
                    for t in range(NTAB):
                        tt = tabs[:, q, t, :].rearrange("p (b f) -> p b f", b=GB)
                        s.link(v.tensor_tensor(agg, cat1[:, q, :, 0:D] if t == 0 else agg, tt, ALU.add))
                    s.link(v.tensor_tensor(cat1[:, q, :, D:], cat1[:, q, :, D:], over(k.rcnt[:, blk], 2, A16), ALU.mult))
                    copy_at(v, cat[:, q, :, 0:D], k.X[:, blk, :]).then_inc(cat_ready, 1)
                    v.wait_ge(cat_ready, 2 * g + 1)
                    v.wait_ge(outp, 2 * g + 1)
                    s.link(v.tensor_tensor(y[:, :, :], psY.rearrange("p (b f) -> p b f", b=GB), cat[:, q, :, 0:D], ALU.add))
                    norm(v, s, y[:, :, :], cat1[:, q, :, 0:D], st, sq[:, :, :], std_in[:, :], std[:, :],
                         lambda: v.wait_ge(root, 2 * g + 1), var, cat_ready)
                    v.wait_ge(outp, 2 * g + 2)
                    s.link(v.tensor_tensor(y[:, :, :], psY.rearrange("p (b f) -> p b f", b=GB), cat1[:, q, :, 0:D], ALU.add))
                    norm(v, s, y[:, :, :], x2[:, :, :], st, sq[:, :, :], std_in[:, :], std[:, :],
                         lambda: v.wait_ge(root, 2 * g + 2), var, rows2)
                    v.wait_ge(rows2, 2 * g + 1)
                    copy_at(v, k.X[:, blk, :], x2[:, :, :]).then_inc(agg_done, 1)
                    for b in range(GB):
                        n = g * GB + b
                        v.wait_ge(ubs, n + 2)
                        if not (is_first(c) and q * GB + b < 2):
                            v.wait_ge(tab_put[(q * GB + b) % 2], 16 * (GB * c + (q * GB + b) // 2))
                        v.tensor_copy(tab[:, (q * GB + b) % 2, 512:], psR[b % 2][:, 512:]).then_inc(tab_ready_v, 1)

            PER = 2 * (1 + NTAB + 1 + 2 * 7)
            turns(v, PAIRS, body, s, PER)


def edges_2(nc, k, ins):
    with ExitStack() as ctx:
        def sb(name, shape, dt=F32):
            return ctx.enter_context(nc.sbuf_tensor(name, shape, dt))

        def sem(name):
            return ctx.enter_context(nc.semaphore(name))

        msg = sb("msg", [P, NS, SL, D])
        run = sb("run2", [P, NS, SL, D])
        idx = sb("idx2", [P, NS, SL], I32)
        same = sb("same2", [P, NS, SL])
        got = [sem(f"msg_got{q}") for q in range(NS)]
        stored = [sem(f"stored2_{q}") for q in range(NS)]
        meta_ready, run_ready, vsteps, zero_put = (
            sem(s) for s in ("meta_ready2", "run_ready2", "vsteps2", "zero_put2"))
        R2 = k.R2[0:E, :].rearrange("(p t) f -> p t f", p=P)
        Z = k.Z[0:E, :].rearrange("(p t) f -> p (t f)", p=P)

        block = ctx.enter_context(nc.Block())

        @block.sync
        def _(sp):
            def body(c):
                for q in range(NS):
                    sp.wait_ge(run_ready, NS * c + q + 1)
                    sp.dma_start(R2[:, bass.ds(c * CH + q * SL, SL), :], run[:, q]).then_inc(stored[q], 16)
                sp.dma_start(Z[:, bass.ds(c * CH * MSG, CH * MSG)], k.zeros[:, 0:CH * MSG]).then_inc(zero_put, 16)

            turns(sp, CHUNKS, body)
            for q in range(NS):
                sp.wait_ge(stored[q], 16 * CHUNKS)
            sp.wait_ge(zero_put, 16 * CHUNKS)

        @block.scalar
        def _(act):
            def body(c):
                for q in range(NS):
                    if not is_first(c):
                        act.wait_ge(run_ready, NS * c + q + 1 - NS)
                    at = bass.ds(c * CH + q * SL, SL)
                    act.copy(idx[:, q], k.rel_i[:, at]).then_inc(meta_ready, 1)
                    act.copy(same[:, q], k.same[:, at]).then_inc(meta_ready, 1)

            turns(act, CHUNKS, body)

        @block.gpsimd
        def _(pool):
            def body(c):
                for q in range(NS):
                    hold(pool, meta_ready, 2 * (NS * c + q + 1), k.passed)
                    for t in range(SL):
                        gather(pool, msg[:, q, t, :], k.Y, idx[:, q, t:t + 1], got[q])

            turns(pool, CHUNKS, body)

        @block.vector
        def _(v):
            s = Steps(v, vsteps)
            s.link(v.memset(run[:, NS - 1, SL - 1, :], 0.0))

            def body(c):
                s.turn(1 + PER * c)
                for q in range(NS):
                    v.wait_ge(got[q], 16 * SL * (c + 1))
                    if not is_first(c):
                        v.wait_ge(stored[q], 16 * c)
                    for t in range(SL):
                        prev = run[:, q, t - 1, :] if t else run[:, (q - 1) % NS, SL - 1, :]
                        if t:
                            s.wait(s.n)
                        elif q or not is_first(c):
                            v.wait_ge(run_ready, NS * c + q)
                        ins_ = v.scalar_tensor_tensor(out=run[:, q, t, :], in0=prev, scalar=same[:, q, t:t + 1],
                                                      in1=msg[:, q, t, :], op0=ALU.mult, op1=ALU.add)
                        if t == SL - 1:
                            ins_.then_inc(run_ready, 1)
                        else:
                            s.done(ins_)

            PER = NS * (SL - 1)
            turns(v, CHUNKS, body, s, PER)
            v.wait_ge(run_ready, CHUNKS * NS)
            v.tensor_copy(k.tail[:, 0:D], run[:, NS - 1, SL - 1, :])

    fix_rows(nc, k, 2, k.R2, D, False)


def nodes_2(nc, k, ins):
    with ExitStack() as ctx:
        def sb(name, shape, dt=F32):
            return ctx.enter_context(nc.sbuf_tensor(name, shape, dt))

        def sem(name):
            return ctx.enter_context(nc.semaphore(name))

        got = sb("got2", [P, 2, GB, D])
        idx = sb("nidx2", [P, 2, GB], I32)
        zidx = sb("zidx", [P, 2, GB], I32)
        y = sb("y2", [P, GB, D])
        sq = sb("sq2", [P, GB, D])
        st = sb("st2", [P, 3, GB])
        std_in = sb("std_in2", [P, GB])
        std = sb("std2", [P, GB])
        x3 = sb("x3", [P, 2, GB, D])
        x3T = sb("x3T", [D, GB * P])
        yz = sb("yz", [P, 2, GB, D])
        first_i = sb("first_i", [P, 1], I32)
        rows_got = [sem(f"rows_got2{q}") for q in range(2)]
        z_put = [sem(f"z_put{q}") for q in range(2)]
        yz_put = [sem(f"yz_put{q}") for q in range(2)]
        idx_ready, zidx_ready, x_ready, turned, turned_c, outp, vsteps, var, root, yz_ready, zi = (
            sem(s) for s in ("idx_ready2", "zidx_ready", "x_ready", "turned2", "turned_c2", "outp2", "nsteps2", "var2",
                             "root2", "yz_ready", "zinit_got"))
        psT, psY = k.psf[0:D, 0:GB * P], k.ps[:, 4, 0:GB * D]
        ytab = k.ytab.rearrange("(p b) f -> p b f", p=P)
        ztab = k.ztab.rearrange("(p b) f -> p b f", p=P)

        block = ctx.enter_context(nc.Block())

        @block.sync
        def _(sp):
            def body(c):
                for q in range(2):
                    g = 2 * c + q
                    sp.wait_ge(yz_ready, g + 1)
                    sp.dma_start(ytab[:, bass.ds(g * GB, GB), :], yz[:, q, :, 0:MSG]).then_inc(yz_put[q], 16)
                    sp.dma_start(ztab[:, bass.ds(g * GB, GB), :], yz[:, q, :, MSG:]).then_inc(yz_put[q], 16)

            turns(sp, PAIRS, body)
            for q in range(2):
                sp.wait_ge(yz_put[q], 32 * PAIRS)

        @block.gpsimd
        def _(pool):
            def body(c):
                for q in range(2):
                    hold(pool, idx_ready, 2 * c + q + 1, k.passed)
                    for b in range(GB):
                        gather(pool, got[:, q, b, :], k.R2, idx[:, q, b:b + 1], rows_got[q])
                for q in range(2):
                    hold(pool, yz_ready, 2 * c + q + 1, k.passed)
                    hold(pool, zidx_ready, 2 * c + q + 1, k.passed)
                    for b in range(GB):
                        scatter(pool, k.Z, zidx[:, q, b:b + 1], yz[:, q, b, MSG:], z_put[q])

            turns(pool, PAIRS, body)
            for q in range(2):
                pool.wait_ge(z_put[q], 16 * GB * PAIRS)
                pool.wait_ge(yz_put[q], 32 * PAIRS)
            pool.wait_ge(zidx_ready, 2 * PAIRS + 1)
            gather(pool, k.zinit[:, :], k.ztab, first_i[:, :], zi)
            pool.wait_ge(zi, 16)

        @block.tensor
        def _(pe):
            def body(c):
                for q in range(2):
                    g = 2 * c + q
                    hold(pe, x_ready, g + 1, k.passed)
                    for b in range(GB):
                        last = nc.tensor.transpose(psT[:, b * P:(b + 1) * P], x3[:, q, b, :], k.ident[:, :])
                    last.then_inc(turned, 1)
                    if not (is_first(c) and q == 0):
                        pe.wait_ge(yz_ready, g)
                    nc.tensor.matmul(psY, k.ones[0:1, :], over(k.b1z[0:1, :], 1, GB), start=True, stop=False)
                    pe.wait_ge(turned_c, g + 1)
                    for b in range(GB):
                        last = nc.tensor.matmul(psY[:, b * D:(b + 1) * D], x3T[:, b * P:(b + 1) * P], k.Wyz[:, :],
                                                start=False, stop=b == GB - 1)
                    last.then_inc(outp, 1)

            turns(pe, PAIRS, body)

        @block.scalar
        def _(act):
            def body(c):
                for q in range(2):
                    g = 2 * c + q
                    act.wait_ge(var, g + 1)
                    act.activation(std[:, :], std_in[:, :], ACT.Sqrt).then_inc(root, 1)
                    act.wait_ge(turned, g + 1)
                    act.copy(x3T[:, :], psT).then_inc(turned_c, 1)
                    act.wait_ge(outp, g + 1)
                    if not is_first(c):
                        act.wait_ge(yz_put[q], 32 * c)
                        act.wait_ge(z_put[q], 16 * GB * c)
                    act.copy(yz[:, q].rearrange("p b f -> p (b f)"), psY).then_inc(yz_ready, 1)

            turns(act, PAIRS, body)

        @block.vector
        def _(v):
            s = Steps(v, vsteps)

            def body(c):
                s.turn(PER * c)
                for q in range(2):
                    g = 2 * c + q
                    blk = bass.ds(g * GB, GB)
                    if not is_first(c):
                        v.wait_ge(x_ready, g - 1)
                        v.wait_ge(z_put[q], 16 * GB * c)
                    copy_at(v, idx[:, q], k.last_i[:, blk]).then_inc(idx_ready, 1)
                    copy_at(v, zidx[:, q], k.zrow_i[:, blk]).then_inc(zidx_ready, 1)
                for q in range(2):
                    g = 2 * c + q
                    blk = bass.ds(g * GB, GB)
                    v.wait_ge(rows_got[q], 16 * GB * (c + 1))
                    s.link(v.tensor_tensor(y[:, :, :], got[:, q], over(k.some[:, blk], 2, D), ALU.mult))
                    s.link(v.tensor_tensor(y[:, :, :], y[:, :, :], k.X[:, blk, :], ALU.add))
                    if not is_first(c):
                        v.wait_ge(turned, g - 1)
                    norm(v, s, y[:, :, :], x3[:, q], st, sq[:, :, :], std_in[:, :], std[:, :],
                         lambda: v.wait_ge(root, g + 1), var)
                    copy_at(v, k.X[:, blk, :], x3[:, q]).then_inc(x_ready, 1)

            PER = 2 * (2 + 7)
            turns(v, PAIRS, body, s, PER)
            v.tensor_copy(first_i[:, :], k.firstf[:, :]).then_inc(zidx_ready, 1)


def edges_3(nc, k, ins):
    with ExitStack() as ctx:
        def sb(name, shape, dt=F32):
            return ctx.enter_context(nc.sbuf_tensor(name, shape, dt))

        def sem(name):
            return ctx.enter_context(nc.semaphore(name))

        W = SL3 * MSG
        ea = sb("ea", [P, NS3, W])
        zs = sb("zs", [P, NS3, W])
        zx = sb("zx", [P, NS3, W])
        yg = sb("yg", [P, NS3, W])
        run = sb("run3", [P, NS3, SL3, 2 * MSG])
        eaT = sb("eaT", [P, LANES, W])
        h1 = sb("h1", [P, LANES, W])
        h2 = sb("h2", [P, LANES, W])
        idx = sb("idx3", [P, NS3, SL3], I32)
        same = sb("same3", [P, NS3, SL3])
        anew = sb("anew", [P, NS3, SL3])
        loaded = [sem(f"loaded3{q}") for q in range(NS3)]
        got = [sem(f"y_got{q}") for q in range(NS3)]
        stored = [sem(f"stored3{q}") for q in range(NS3)]
        idx_ready, turned, turned_c, pre, pre_r, mid, mid_r, fin, zready, run_ready, vsteps = (
            sem(s) for s in ("idx_ready3e", "turned3", "turned_c3", "pre", "pre_r", "mid", "mid_r", "fin", "zready",
                             "run_ready3", "vsteps3"))
        e32 = ins["edge_attr_32"].rearrange("(p t) f -> p (t f)", p=P)
        Z = k.Z[0:E, :].rearrange("(p t) f -> p (t f)", p=P)
        R3 = k.R3[0:E, :].rearrange("(p t) f -> p t f", p=P)
        LAST = CHUNKS3 - 1

        def ps(stage, q):
            return k.ps[:, LANES * stage + q % LANES, 0:W]

        def groups(steps):
            return [(4 * MSG * g, min(4, steps - 4 * g) * MSG) for g in range(-(-steps // 4))]

        def cuts(steps):
            return [(0, W, P)] if steps == SL3 else [(a, a + P, w) for a, w in groups(steps)]

        def lags(c, q, n):
            return not is_first(c) or q >= n

        block = ctx.enter_context(nc.Block())

        @block.sync
        def _(sp):
            def load(c, q, steps=SL3):
                at = bass.ds((c * CH3 + q * SL3) * MSG, steps * MSG)
                sp.dma_start(ea[:, q, 0:steps * MSG], e32[:, at]).then_inc(loaded[q], 16)
                sp.dma_start(zs[:, q, 0:steps * MSG], Z[:, at]).then_inc(loaded[q], 16)

            def store(c, q, steps=SL3):
                sp.wait_ge(run_ready, NS3 * c + q + 1)
                sp.dma_start(R3[:, bass.ds(c * CH3 + q * SL3, steps), :], run[:, q, 0:steps]).then_inc(stored[q], 16)

            def free(n):
                sp.wait_ge(turned, n + 1)
                sp.wait_ge(zready, n + 1)

            for q in range(NS3):
                load(0, q)
            with sp.Fori(0, LAST) as c:
                for q in range(NS3):
                    free(NS3 * c + q)
                    load(c + 1, q)
                    store(c, q)
            for q in range(NS3):
                if q < len(TAILS3):
                    free(NS3 * LAST + q)
                    load(CHUNKS3, q, TAILS3[q])
                store(LAST, q)
            for q, steps in enumerate(TAILS3):
                store(CHUNKS3, q, steps)
            for q in range(NS3):
                sp.wait_ge(stored[q], 16 * (CHUNKS3 + (q < len(TAILS3))))

        @block.gpsimd
        def _(pool):
            def slot(c, q, steps):
                hold(pool, idx_ready, NS3 * c + q + 1, k.passed)
                if not is_first(c):
                    hold(pool, pre, NS3 * c + q + 1 - NS3, k.passed)
                for t in range(steps):
                    gather(pool, yg[:, q, t * MSG:(t + 1) * MSG], k.ytab, idx[:, q, t:t + 1], got[q])

            def body(c):
                for q in range(NS3):
                    slot(c, q, SL3)

            turns(pool, CHUNKS3, body)
            for q, steps in enumerate(TAILS3):
                slot(CHUNKS3, q, steps)

        @block.tensor
        def _(pe):
            def slot(c, q, steps):
                n, m = NS3 * c + q, q % LANES
                behind = lags(c, q, LANES)
                pe.wait_ge(loaded[q], 32 * c + 32)
                if behind:
                    pe.wait_ge(turned_c, n + 1 - LANES)
                for a, w in groups(steps):
                    last = nc.tensor.transpose(ps(0, q)[0:w, a:a + P], ea[:, q, a:a + w], k.ident[:, :])
                last.then_inc(turned, 1)
                if behind:
                    pe.wait_ge(pre_r, n + 1 - LANES)
                pe.wait_ge(turned_c, n + 1)
                pe.wait_ge(zready, n + 1)
                pe.wait_ge(got[q], 16 * SL3 * c + 16 * steps)
                for a, b, w in cuts(steps):
                    nc.tensor.matmul(ps(1, q)[0:w, a:b], k.W1e[0:w, 0:w], eaT[0:w, m, a:b], start=True, stop=False)
                    for g, _ in groups(steps):
                        if a <= g < b:
                            nc.tensor.matmul(ps(1, q)[0:w, g:g + P], zx[:, q, g:g + w], k.ident[:, :],
                                             start=False, stop=False)
                            last = nc.tensor.matmul(ps(1, q)[0:w, g:g + P], yg[:, q, g:g + w], k.ident[:, :],
                                                    start=False, stop=g + P >= b)
                last.then_inc(pre, 1)
                if behind:
                    pe.wait_ge(mid_r, n + 1 - LANES)
                pe.wait_ge(pre_r, n + 1)
                for a, b, w in cuts(steps):
                    last = nc.tensor.matmul(ps(2, q)[0:w, a:b], k.W2e[0:w, 0:w], h1[0:w, m, a:b], start=True, stop=True)
                last.then_inc(mid, 1)
                if behind:
                    pe.wait_ge(run_ready, n + 1 - LANES)
                pe.wait_ge(mid_r, n + 1)
                for a, w in groups(steps):
                    last = nc.tensor.matmul(ps(3, q)[:, a:a + w], h2[0:w, m, a:a + P], k.W3e[0:w, 0:w],
                                            start=True, stop=True)
                last.then_inc(fin, 1)

            def body(c):
                for q in range(NS3):
                    slot(c, q, SL3)

            turns(pe, CHUNKS3, body)
            for q, steps in enumerate(TAILS3):
                slot(CHUNKS3, q, steps)

        @block.scalar
        def _(act):
            def copy_idx(c, q):
                act.copy(idx[:, q, :], k.src[:, bass.ds(c * CH3 + q * SL3, SL3)]).then_inc(idx_ready, 1)

            def slot(c, q, steps):
                n, m = NS3 * c + q, q % LANES
                behind = lags(c, q, LANES)
                act.wait_ge(turned, n + 1)
                if behind:
                    act.wait_ge(pre, n + 1 - LANES)
                for a, b, w in cuts(steps):
                    last = act.copy(eaT[0:w, m, a:b], ps(0, q)[0:w, a:b])
                last.then_inc(turned_c, 1)
                act.wait_ge(pre, n + 1)
                if behind:
                    act.wait_ge(mid, n + 1 - LANES)
                for a, b, w in cuts(steps):
                    last = act.activation(h1[0:w, m, a:b], ps(1, q)[0:w, a:b], ACT.Relu)
                last.then_inc(pre_r, 1)
                if steps == SL3 and not (isinstance(c, int) and c == CHUNKS3):
                    copy_idx(c + 1, q)
                act.wait_ge(mid, n + 1)
                if behind:
                    act.wait_ge(fin, n + 1 - LANES)
                for a, b, w in cuts(steps):
                    last = act.activation(h2[0:w, m, a:b], ps(2, q)[0:w, a:b], ACT.Relu, bias=k.b2e[0:w, 0:1])
                last.then_inc(mid_r, 1)

            def body(c):
                for q in range(NS3):
                    slot(c, q, SL3)

            for q in range(NS3):
                copy_idx(0, q)
            turns(act, CHUNKS3, body)
            for q, steps in enumerate(TAILS3):
                slot(CHUNKS3, q, steps)

        @block.vector
        def _(v):
            s = Steps(v, vsteps)
            s.link(v.memset(run[:, NS3 - 1, SL3 - 1, :], 0.0))

            def meta(c, q):
                at = bass.ds(c * CH3 + q * SL3, SL3)
                s.done(copy_at(v, same[:, q, :], k.same[:, at]))
                s.done(v.tensor_scalar(anew[:, q, :], k.same[:, at], 1.0, HUGE, ALU.subtract, ALU.mult))

            def spread_z(c, q, steps):
                n = NS3 * c + q
                v.wait_ge(loaded[q], 32 * c + 32)
                if not is_first(c):
                    v.wait_ge(pre, n + 1 - NS3)
                if lags(c, q, 1):
                    v.wait_ge(zready, n)
                for t in range(steps):
                    o = zx[:, q, t * MSG:(t + 1) * MSG]
                    if is_first(c) and q == 0 and t == 0:
                        last = v.tensor_copy(o, k.zinit[:, :])
                    else:
                        p = zx[:, q, (t - 1) * MSG:t * MSG] if t else zx[:, (q - 1) % NS3, W - MSG:]
                        last = v.scalar_tensor_tensor(out=o, in0=p, scalar=same[:, q, t:t + 1],
                                                      in1=zs[:, q, t * MSG:(t + 1) * MSG], op0=ALU.mult, op1=ALU.add)
                    if t < steps - 1:
                        s.link(last)
                    else:
                        last.then_inc(zready, 1)

            def aggregate(c, q, steps):
                n = NS3 * c + q
                v.wait_ge(fin, n + 1)
                if not is_first(c):
                    v.wait_ge(stored[q], 16 * c)
                if lags(c, q, 1):
                    v.wait_ge(run_ready, n)
                for t in range(steps):
                    h = ps(3, q)[:, t * MSG:(t + 1) * MSG]
                    p = run[:, q, t - 1, :] if t else run[:, (q - 1) % NS3, SL3 - 1, :]
                    s.done(v.scalar_tensor_tensor(out=run[:, q, t, 0:MSG], in0=p[:, 0:MSG], scalar=same[:, q, t:t + 1],
                                                  in1=h, op0=ALU.mult, op1=ALU.add))
                    b = v.scalar_tensor_tensor(out=run[:, q, t, MSG:], in0=p[:, MSG:], scalar=anew[:, q, t:t + 1],
                                               in1=h, op0=ALU.add, op1=ALU.max)
                    if t < steps - 1:
                        s.link(b)
                    else:
                        b.then_inc(run_ready, 1)

            def body(c):
                s.turn(BEFORE + PER * c)
                for q in range(NS3):
                    spread_z(c + (q + 1) // NS3, (q + 1) % NS3, SL3)
                    aggregate(c, q, SL3)
                    v.wait_ge(run_ready, NS3 * c + q + 1)
                    meta(c + 1, q)

            PER = NS3 * (3 * SL3 - 2 + 2)
            for q in range(NS3):
                meta(0, q)
            s.wait(s.n)
            spread_z(0, 0, SL3)
            BEFORE = s.n
            turns(v, CHUNKS3, body, s, PER)
            s.turn(BEFORE + PER * CHUNKS3)
            for q, steps in enumerate(TAILS3):
                if q + 1 < len(TAILS3):
                    spread_z(CHUNKS3, q + 1, TAILS3[q + 1])
                aggregate(CHUNKS3, q, steps)
            v.wait_ge(run_ready, CHUNKS3 * NS3 + len(TAILS3))
            v.tensor_copy(k.tail[:, 0:2 * MSG], run[:, len(TAILS3) - 1, TAILS3[-1] - 1, :])

    fix_rows(nc, k, 3, k.R3, 2 * MSG, True)


def nodes_3(nc, k, ins, out):
    with ExitStack() as ctx:
        def sb(name, shape, dt=F32):
            return ctx.enter_context(nc.sbuf_tensor(name, shape, dt))

        def sem(name):
            return ctx.enter_context(nc.semaphore(name))

        got = sb("got3", [P, 2, GB, 2 * MSG])
        idx = sb("nidx3", [P, 2, GB], I32)
        cat = sb("cat3", [P, 2, GB, HID])
        catT = sb("catT3", [P, GB * P])
        h1 = sb("nh1", [MSG, GB * P])
        h2 = sb("nh2", [MSG, GB * P])
        y = sb("y3", [P, GB, D])
        sq = sb("sq3", [P, GB, D])
        st = sb("st3", [P, 3, GB])
        std_in = sb("std_in3", [P, GB])
        std = sb("std3", [P, GB])
        ub = sb("ub3", [MSG, 1])
        rows_got = [sem(f"rows_got3{q}") for q in range(2)]
        idx_ready, cat_ready, turned, turned_c, hid, hid_r, hid2, hid2_r, outp, vsteps, var, root, ubs, ub_ready, y_ready, saved = (
            sem(s) for s in ("idx_ready3", "cat_ready3", "turned4", "turned_c4", "hid3", "hid_r3", "hid23", "hid2_r3",
                             "outp3", "nsteps3", "var3", "root3", "ubs3", "ub_ready3", "y_ready3", "saved"))
        psT, psH, psH2 = k.psf[:, 0:GB * P], k.psf[0:MSG, 1024:1024 + GB * P], k.psf[0:MSG, 2048:2048 + GB * P]
        psY = k.ps[:, 6, 0:GB * D]
        halves = ((0, 512), (512, GB * P))

        block = ctx.enter_context(nc.Block())

        @block.sync
        def _(sp):
            sp.wait_ge(y_ready, 2 * PAIRS)
            sp.dma_start(out[0:LASTP * NB, :].rearrange("(p b) f -> p b f", b=NB), k.X[0:LASTP, :, :]).then_inc(saved, 16)
            sp.dma_start(out[LASTP * NB:N, :].rearrange("(p b) f -> p b f", p=1),
                         k.X[LASTP:LASTP + 1, 0:LASTN, :]).then_inc(saved, 16)
            sp.wait_ge(saved, 32)

        @block.gpsimd
        def _(pool):
            def body(c):
                for q in range(2):
                    hold(pool, idx_ready, 2 * c + q + 1, k.passed)
                    for b in range(GB):
                        gather(pool, got[:, q, b, :], k.R3, idx[:, q, b:b + 1], rows_got[q])

            turns(pool, PAIRS, body)

        @block.tensor
        def _(pe):
            nc.tensor.matmul(k.ps[0:MSG, 7, 0:1], k.W4u[:, :], k.u3[:, :], start=True, stop=True).then_inc(ubs, 1)

            def body(c):
                for q in range(2):
                    g = 2 * c + q
                    pe.wait_ge(cat_ready, g + 1)
                    for b in range(GB):
                        last = nc.tensor.transpose(psT[:, b * P:(b + 1) * P], cat[:, q, b, :], k.ident[:, :])
                    last.then_inc(turned, 1)
                    pe.wait_ge(turned_c, g + 1)
                    for a, z in halves:
                        last = nc.tensor.matmul(psH[:, a:z], k.W4a[:, :], catT[:, a:z], start=True, stop=True)
                    last.then_inc(hid, 1)
                    hold(pe, hid_r, g + 1, k.passed)
                    for a, z in halves:
                        last = nc.tensor.matmul(psH2[:, a:z], k.W5[:, :], h1[:, a:z], start=True, stop=True)
                    last.then_inc(hid2, 1)
                    if not (is_first(c) and q == 0):
                        pe.wait_ge(y_ready, g)
                    nc.tensor.matmul(psY, k.ones[0:1, :], over(k.b6[0:1, :], 1, GB), start=True, stop=False)
                    hold(pe, hid2_r, g + 1, k.passed)
                    for b in range(GB):
                        last = nc.tensor.matmul(psY[:, b * D:(b + 1) * D], h2[:, b * P:(b + 1) * P], k.W6[:, :],
                                                start=False, stop=b == GB - 1)
                    last.then_inc(outp, 1)

            turns(pe, PAIRS, body)

        @block.scalar
        def _(act):
            def body(c):
                for q in range(2):
                    g = 2 * c + q
                    act.wait_ge(turned, g + 1)
                    for a, z in halves:
                        last = act.copy(catT[:, a:z], psT[:, a:z])
                    last.then_inc(turned_c, 1)
                    act.wait_ge(hid, g + 1)
                    for a, z in halves:
                        last = act.activation(h1[:, a:z], psH[:, a:z], ACT.Relu, bias=ub[:, 0:1])
                    last.then_inc(hid_r, 1)
                    act.wait_ge(hid2, g + 1)
                    for a, z in halves:
                        last = act.activation(h2[:, a:z], psH2[:, a:z], ACT.Relu, bias=k.b5[:, 0:1])
                    last.then_inc(hid2_r, 1)
                    act.wait_ge(var, g + 1)
                    act.activation(std[:, :], std_in[:, :], ACT.Sqrt).then_inc(root, 1)

            act.wait_ge(ubs, 1)
            act.activation(ub[:, :], k.ps[0:MSG, 7, 0:1], ACT.Identity, bias=k.b4[:, 0:1]).then_inc(ub_ready, 1)
            act.wait_ge(ub_ready, 1)
            turns(act, PAIRS, body)

        @block.vector
        def _(v):
            s = Steps(v, vsteps)

            def prepare(c, q):
                g = 2 * c + q
                blk = bass.ds(g * GB, GB)
                v.wait_ge(rows_got[q], 16 * GB * (c + 1))
                if not is_first(c):
                    v.wait_ge(turned, g - 1)
                ne = over(k.some[:, blk], 2, MSG)
                b3 = over(k.b3[:, :], 1, GB)
                mean, peak = cat[:, q, :, D:D + MSG], cat[:, q, :, D + MSG:]
                s.done(v.tensor_tensor(mean, got[:, q, :, 0:MSG], over(k.rcnt[:, blk], 2, MSG), ALU.mult))
                s.done(v.tensor_tensor(peak, got[:, q, :, MSG:], b3, ALU.add))
                s.wait(s.n)
                s.link(v.tensor_tensor(mean, mean, b3, ALU.add))
                s.done(v.tensor_tensor(mean, mean, ne, ALU.mult))
                s.done(v.tensor_tensor(peak, peak, ne, ALU.mult))
                copy_at(v, cat[:, q, :, 0:D], k.X[:, blk, :]).then_inc(cat_ready, 1)

            def body(c):
                s.turn(PER * c)
                for q in range(2):
                    copy_at(v, idx[:, q], k.last_i[:, bass.ds((2 * c + q) * GB, GB)]).then_inc(idx_ready, 1)
                for q in range(2):
                    prepare(c, q)
                for q in range(2):
                    g = 2 * c + q
                    v.wait_ge(outp, g + 1)
                    s.link(v.tensor_tensor(y[:, :, :], psY.rearrange("p (b f) -> p b f", b=GB), cat[:, q, :, 0:D], ALU.add))
                    norm(v, s, y[:, :, :], k.X[:, bass.ds(g * GB, GB), :], st, sq[:, :, :], std_in[:, :], std[:, :],
                         lambda: v.wait_ge(root, g + 1), var, y_ready)

            PER = 2 * (5 + 1 + 6)
            turns(v, PAIRS, body, s, PER)


def build(nc, ins, out):
    with ExitStack() as ctx:
        k = Kernel()

        def sb(name, shape, dt=F32):
            return ctx.enter_context(nc.sbuf_tensor(name, shape, dt))

        def dram(name, shape, dt=F32):
            return nc.dram_tensor(name, shape, dt, kind="Internal").ap()

        k.ps = ctx.enter_context(nc.psum_tensor("ps", [P, 8, 512], F32))
        k.psf = k.ps[:, :, :].rearrange("p a b -> p (a b)")
        k.X = sb("X", [P, NB, D])
        k.nid, k.some, k.rcnt = (sb(s, [P, NB]) for s in ("nid", "some", "rcnt"))
        k.last_i, k.zrow_i = (sb(s, [P, NB], I32) for s in ("last_i", "zrow_i"))
        k.src, k.same, k.dump = (sb(s, [P, T + CH]) for s in ("src_f", "same_f", "dump_f"))
        k.rel_i = sb("rel_i", [P, T], I32)
        k.firstf, k.fix_i, k.tail = sb("firstf", [P, 1]), sb("fix_i", [P, 1], I32), sb("tail", [P, R1W])
        k.before, k.chain, k.joins = sb("before", [P, P]), sb("chain", [MSG, P]), sb("joins", [MSG, P])
        k.zinit = sb("zinit", [P, MSG])
        k.ident, k.upper, k.ones = sb("ident", [P, P]), sb("upper", [P, 4, P]), sb("ones", [1, P])
        k.zeros = sb("zeros", [P, TABR * D // P // 4])
        k.W1a, k.W2a, k.b1a, k.b2a = sb("W1a", [HID, HID]), sb("W2a", [HID, D]), sb("b1a", [HID, 1]), sb("b2a", [1, D])
        k.W1b, k.W1bu, k.u1 = sb("W1b", [R1W, HID]), sb("W1bu", [D, HID]), sb("u1", [D, 1])
        k.W2b, k.b1b, k.b2b = sb("W2b", [HID, D]), sb("b1b", [HID, 1]), sb("b2b", [1, D])
        k.W2r = sb("W2r", [D, RELS, D])
        k.Wyz, k.b1z = sb("Wyz", [D, D]), sb("b1z", [1, D])
        k.W1e, k.W2e, k.W3e, k.b2e, k.b3 = (sb("W1e", [P, P]), sb("W2e", [P, P]), sb("W3e", [P, P]),
                                            sb("b2e", [P, 1]), sb("b3", [P, MSG]))
        k.W4a, k.W4u, k.u3, k.b4 = sb("W4a", [HID, MSG]), sb("W4u", [MSG, MSG]), sb("u3", [MSG, 1]), sb("b4", [MSG, 1])
        k.W5, k.b5, k.W6, k.b6 = sb("W5", [MSG, MSG]), sb("b5", [MSG, 1]), sb("W6", [MSG, D]), sb("b6", [1, D])

        def w(name, n=3):
            return ins[f"L{n}_gnn_{name}"]

        def col(a):
            return a.rearrange("(n a) -> n a", a=1)

        def row(a):
            return a.rearrange("(a n) -> a n", a=1)

        k.loads = [
            (k.W1a[:, :], w("W1", 0)), (k.W2a[:, :], w("W2", 0)), (k.b1a[:, :], col(w("b1", 0))), (k.b2a[:, :], row(w("b2", 0))),
            (k.W1b[:, :], w("W1", 1)[0:R1W, :]), (k.W1bu[:, :], w("W1", 1)[R1W:, :]), (k.u1[:, :], w("u", 1)[0:1, :].rearrange("a n -> n a")),
            (k.W2b[:, :], w("W2", 1)), (k.b1b[:, :], col(w("b1", 1))), (k.b2b[:, :], row(w("b2", 1))),
            (k.W2r[:, :, :], w("weight", 2).rearrange("r i o -> i r o")),
            (k.Wyz[:, 0:MSG], w("W1")[0:D, :]), (k.Wyz[:, MSG:], w("W1")[D:2 * D, :]), (k.b1z[:, MSG:], row(w("b1"))),
            (k.b3[:, :], row(w("b3")).to_broadcast([P, MSG])),
            (k.W4a[:, :], w("W4")[0:HID, :]), (k.W4u[:, :], w("W4")[HID:, :]), (k.u3[:, :], w("u")[0:1, :].rearrange("a n -> n a")),
            (k.b4[:, :], col(w("b4"))), (k.W5[:, :], w("W5")), (k.b5[:, :], col(w("b5"))), (k.W6[:, :], w("W6")), (k.b6[:, :], row(w("b6"))),
        ]
        for j in range(4):
            d = slice(j * MSG, (j + 1) * MSG)
            k.loads += [(k.W1e[d, d], w("W1")[2 * D:, :]), (k.W2e[d, d], w("W2")), (k.W3e[d, d], w("W3")), (k.b2e[d, :], col(w("b2")))]

        k.coarse_d, k.ends = dram("coarse_d", [CR]), dram("ends", [NP + 1, 1], I32)
        k.tables = [dram(f"table{t}", [TABR, D]) for t in range(NTAB)]
        k.R1, k.R2, k.R3 = dram("R1", [E + P, R1W]), dram("R2", [E + P, D]), dram("R3", [E + P, 2 * MSG])
        k.Y = dram("Y", [NP * RELS, D])
        k.ytab, k.ztab, k.Z = dram("ytab", [NP, MSG]), dram("ztab", [NP, MSG]), dram("Z", [E + NP, MSG])

        k.passed = ctx.enter_context(nc.semaphore("passed"))
        setup(nc, k, ins)
        edges_01(nc, k, ins)
        nodes_01(nc, k, ins)
        edges_2(nc, k, ins)
        nodes_2(nc, k, ins)
        edges_3(nc, k, ins)
        nodes_3(nc, k, ins, out)


_INS = ['x', 'src', 'dst', 'edge_attr_16', 'edge_attr_32', 'edge_attr_64', 'edge_type_16',
        'L0_gnn_W1', 'L0_gnn_b1', 'L0_gnn_W2', 'L0_gnn_b2', 'L1_gnn_u', 'L1_gnn_W1', 'L1_gnn_b1', 'L1_gnn_W2',
        'L1_gnn_b2', 'L2_gnn_weight', 'L3_gnn_u', 'L3_gnn_W1', 'L3_gnn_b1', 'L3_gnn_W2', 'L3_gnn_b2', 'L3_gnn_W3',
        'L3_gnn_b3', 'L3_gnn_W4', 'L3_gnn_b4', 'L3_gnn_W5', 'L3_gnn_b5', 'L3_gnn_W6', 'L3_gnn_b6']


def kernel(**inputs):
    import numpy as np
    import concourse.bacc as bacc
    from concourse.bass_utils import run_bass_kernel_spmd

    nc = bacc.Bacc("TRN2", target_bir_lowering=False, num_devices=1)
    arrays, ins = {}, {}
    for name in _INS:
        a = np.ascontiguousarray(inputs[name])
        arrays[f"in_{name}"] = a
        ins[name] = nc.dram_tensor(f"in_{name}", a.shape, mybir.dt.from_np(a.dtype), kind="ExternalInput").ap()
    out = nc.dram_tensor("out", (N, D), F32, kind="ExternalOutput").ap()
    build(nc, ins, out)
    r = run_bass_kernel_spmd(nc, [arrays], core_ids=[0])
    return r.results[0]["out"]
```

```python
import concourse.bass as bass
from concourse import mybir
from contextlib import ExitStack

F32 = mybir.dt.float32
BF16 = mybir.dt.bfloat16
I32 = mybir.dt.int32
ALU = mybir.AluOpType
ACT = mybir.ActivationFunctionType
AX = mybir.AxisListType

P = 128
N = 12500
E = 400000
T = E // P
NB = -(-N // P)
NP = NB * P
LASTP = N // NB
LASTN = N - LASTP * NB
D = 64
A16 = 16
R1W = D + A16
HID = 128
RELS = 16
MSG = 32
SL = 5
NS = 5
CH = SL * NS
CHUNKS = T // CH
SL3 = 8
NS3 = 4
CH3 = SL3 * NS3
CHUNKS3 = T // CH3
TAIL3 = T - CHUNKS3 * CH3
TAILS3 = [min(SL3, TAIL3 - a) for a in range(0, TAIL3, SL3)]
LANES = 2
NTAB = SL
TABR = NP + P
GB = 7
PAIRS = NB // (2 * GB)
CR, CC = 640, 625
BIG = float(2 ** 20)
HUGE = 3.0e38
EPS = 1e-5


class Steps:

    def __init__(self, eng, sem):
        self.eng, self.sem, self.base, self.n = eng, sem, 0, 0

    def turn(self, base):
        self.base, self.n = base, 0

    def done(self, ins):
        ins.then_inc(self.sem, 1)
        self.n += 1
        return self.n

    def wait(self, n):
        self.eng.wait_ge(self.sem, self.base + n)

    def link(self, ins):
        self.wait(self.done(ins))


def is_first(c):
    return isinstance(c, int) and c == 0


def turns(eng, n, body, steps=None, per=0):
    body(0)
    assert steps is None or steps.n == per, (steps.n, per)
    with eng.Fori(1, n) as c:
        body(c)


def turns_ahead(eng, n, body, steps=None, per=0):
    body(0, True)
    assert steps is None or steps.n == per, (steps.n, per)
    with eng.Fori(1, n - 1) as c:
        body(c, True)
    body(n - 1, False)


def hold(eng, sem, n, passed):
    eng.wait_ge(sem, n)
    if not isinstance(n, int):
        eng.sem_inc(passed, 1)


def copy_at(v, out, in_):
    return v.tensor_scalar(out, in_, 1.0, None, ALU.mult)


def gather(eng, out, table, index, sem):
    eng.indirect_dma_start(out=out, out_offset=None, in_=table,
                           in_offset=bass.IndirectOffsetOnAxis(ap=index, axis=0)).then_inc(sem, 16)


def scatter(eng, table, index, in_, sem, add=False):
    kw = {"compute_op": ALU.add} if add else {}
    eng.indirect_dma_start(out=table, out_offset=bass.IndirectOffsetOnAxis(ap=index, axis=0),
                           in_=in_, in_offset=None, **kw).then_inc(sem, 16)


def over(ap, axis, n):
    return ap.unsqueeze(axis).to_broadcast([*ap.shape[:axis], n, *ap.shape[axis:]])


class Kernel:
    pass


def setup(nc, k, ins):
    with ExitStack() as ctx:
        def sb(name, shape, dt=F32):
            return ctx.enter_context(nc.sbuf_tensor(name, shape, dt))

        def sem(name):
            return ctx.enter_context(nc.semaphore(name))

        dst_i = sb("dst_i", [P, T], I32)
        src_i = sb("src_raw", [P, T], I32)
        typ_i = sb("typ_i", [P, T], I32)
        dst_f = sb("dst_f", [P, T])
        coarse5 = sb("coarse5", [P, CR // P], I32)
        coarse5f = sb("coarse5f", [P, CR // P])
        coarse = sb("coarse", [P, CR])
        junk, junk_act = sb("junk", [P, CR]), sb("junk_act", [P, 2, CR])
        rows = sb("rows", [P, 2, GB, CC], I32)
        nid_i, nid = sb("nid_i", [P, NB + 2 * GB], I32), sb("nid", [P, NB + 2 * GB])
        ncol, nhalf, rsum = (sb(s, [P, 2, GB]) for s in ("ncol", "nhalf", "rsum"))
        rcount = sb("rcount", [P, 2, GB])
        rfound = sb("rfound", [P, 2, GB])
        row_i = sb("row_i", [P, 2, GB], I32)
        end_f = sb("end_f", [P, NB])
        end_i = sb("end_i", [P, NB], I32)
        start_i = sb("start_i", [P, NB], I32)
        start_f = sb("start_f", [P, NB])
        cnt = sb("cnt", [P, NB])
        tmp = sb("tmp", [P, NB])
        pid_i = sb("pid_i", [P, 1], I32)
        pid = sb("pid", [P, 1])
        fend_i = sb("fend_i", [P, 1], I32)
        fidx = sb("fidx", [P, 1], I32)
        fend = sb("fend", [P, 1])
        cols = sb("cols", [P, 4])
        bigsel = sb("bigsel", [P, P])
        lastr = sb("lastr", [MSG, P])
        firstr = sb("firstr", [MSG, P])
        one_i = sb("one_i", [1, 1], I32)
        l_idx, l_c5, l_co, settled = (sem(s) for s in ("l_idx", "l_c5", "l_co", "settled"))
        consts, wzero = sem("consts"), sem("wzero")
        c5_ready, c5_saved, row_ready = sem("c5_ready"), sem("c5_saved"), sem("row_ready")
        row_got = [sem(f"row_got{q}") for q in range(2)]
        ncol_ready, counted = sem("ncol_ready"), sem("counted")
        end_ready, ends_moved, fend_got, one_ready = sem("end_ready"), sem("ends_moved"), sem("fend_got"), sem("one_ready")
        steps, rows_built, search = sem("setup_steps"), sem("rows_built"), sem("search_steps")
        psS = k.ps[:, 0, 0:P]
        psL = k.ps[0:MSG, 1, 0:P]
        psF = k.ps[0:MSG, 2, 0:P]
        nodes = k.X[0:LASTP, :, :]
        NW = len(k.loads)

        block = ctx.enter_context(nc.Block())

        @block.sync
        def _(sp):
            sp.dma_start(coarse5[:, :], ins["dst"].rearrange("(p j c) -> p j c", p=P, c=CC)[:, :, 0],
                         allow_slow_non_contiguous=True).then_inc(l_c5, 16)
            sp.wait_ge(c5_ready, 1)
            sp.dma_start(k.coarse_d.rearrange("(p j) -> p j", p=P), coarse5f[:, :]).then_inc(c5_saved, 16)
            sp.wait_ge(c5_saved, 16)
            sp.dma_start(coarse[:, :], k.coarse_d.rearrange("(a n) -> a n", a=1).to_broadcast([P, CR])).then_inc(l_co, 16)
            sp.dma_start(dst_i[:, :], ins["dst"].rearrange("(p t) -> p t", p=P)).then_inc(l_idx, 16)
            sp.dma_start(src_i[:, :], ins["src"].rearrange("(p t) -> p t", p=P)).then_inc(l_idx, 16)
            sp.dma_start(typ_i[:, :], ins["edge_type_16"].rearrange("(p t) -> p t", p=P)).then_inc(l_idx, 16)
            sp.wait_ge(wzero, 6)
            sp.dma_start(nodes, ins["x"][0:LASTP * NB, :].rearrange("(p b) f -> p b f", b=NB)).then_inc(settled, 16)
            sp.dma_start(k.X[LASTP:LASTP + 1, 0:LASTN, :],
                         ins["x"][LASTP * NB:N, :].rearrange("(p b) f -> p b f", p=1)).then_inc(settled, 16)
            for dst, src in k.loads:
                sp.dma_start(dst, src, allow_slow_non_contiguous=True).then_inc(settled, 16)
            for tab in k.tables:
                flat = tab.rearrange("(p a) f -> p (a f)", p=P)
                w = TABR * D // P
                for q in range(4):
                    sp.dma_start(flat[:, q * w // 4:(q + 1) * w // 4], k.zeros[:, 0:w // 4]).then_inc(settled, 16)
            for r, w in ((k.R1, R1W), (k.R2, D), (k.R3, D)):
                sp.dma_start(r[E:E + P, :], k.zeros[:, 0:w]).then_inc(settled, 16)
            sp.wait_ge(one_ready, 1)
            sp.dma_start(k.ends[0:1, :], one_i[:, :]).then_inc(ends_moved, 16)
            sp.wait_ge(end_ready, 1)
            sp.dma_start(k.ends[1:NP + 1, :].rearrange("(p b) a -> p (b a)", b=NB), end_i[:, :]).then_inc(ends_moved, 16)
            sp.wait_ge(ends_moved, 32)
            sp.dma_start(start_i[:, :], k.ends[0:NP, :].rearrange("(p b) a -> p (b a)", b=NB)).then_inc(ends_moved, 16)
            sp.wait_ge(settled, 16 * (2 + NW + 4 * NTAB + 3))

        @block.gpsimd
        def _(pool):
            pool.memset(k.ident[:, :], 0.0).then_inc(consts, 1)
            pool.memset(k.upper[:, :, :], 0.0).then_inc(consts, 1)
            pool.memset(bigsel[:, :], 0.0).then_inc(consts, 1)
            pool.wait_ge(consts, 3)
            pool.affine_select(out=k.ident[:, :], in_=k.ident[:, :], compare_op=ALU.not_equal, fill=1.0,
                               base=0, pattern=[[-1, P]], channel_multiplier=1).then_inc(consts, 1)
            pool.affine_select(out=k.upper[:, :, :], in_=k.upper[:, :, :], compare_op=ALU.is_ge, fill=BIG,
                               base=0, pattern=[[0, 4], [1, P]], channel_multiplier=-1).then_inc(consts, 1)
            pool.affine_select(out=bigsel[:, :], in_=bigsel[:, :], compare_op=ALU.is_ge, fill=BIG,
                               base=-1, pattern=[[1, P]], channel_multiplier=-1).then_inc(consts, 1)
            pool.iota(nid_i[:, :], pattern=[[1, NB + 2 * GB]], base=0, channel_multiplier=NB).then_inc(consts, 1)
            pool.iota(pid_i[:, :], pattern=[[1, 1]], base=0, channel_multiplier=1).then_inc(consts, 1)
            pool.memset(one_i[:, :], 0).then_inc(one_ready, 1)
            def body(c):
                for q in range(2):
                    hold(pool, row_ready, 2 * c + q + 1, k.passed)
                    for b in range(GB):
                        gather(pool, rows[:, q, b, :], ins["dst"].rearrange("(r c) -> r c", c=CC),
                               row_i[:, q, b:b + 1], row_got[q])

            turns(pool, PAIRS, body)
            pool.wait_ge(ends_moved, 32)
            gather(pool, fend_i[:, :], k.ends, fidx[:, :], fend_got)

        @block.tensor
        def _(pe):
            pe.wait_ge(consts, 8)
            pe.wait_ge(steps, 8)
            nc.tensor.matmul(psS, cols[:, 0:1].to_broadcast([P, P]), k.ident[:, :], start=True, stop=False)
            nc.tensor.matmul(psS, k.ident[:, :], bigsel[:, :], start=False, stop=True)
            nc.tensor.matmul(psL, cols[:, 1:2].to_broadcast([P, MSG]), k.ident[:, :], start=True, stop=True)
            nc.tensor.matmul(psF, cols[:, 0:1].to_broadcast([P, MSG]), k.ident[:, :], start=True, stop=True)\
                .then_inc(rows_built, 1)

        @block.scalar
        def _(act):
            act.wait_ge(l_co, 16)
            def body(c):
                for q in range(2):
                    act.wait_ge(ncol_ready, 2 * c + q + 1)
                    for b in range(GB):
                        if not is_first(c) or q * GB + b > 1:
                            act.wait_ge(counted, (2 * c + q) * GB + b - 1)
                        act.activation(junk_act[:, (q * GB + b) % 2, :], coarse[:, :],
                                       ACT.Sign, scale=-1.0, bias=nhalf[:, q, b:b + 1],
                                       accum_out=rsum[:, q, b:b + 1]).then_inc(counted, 1)

            turns(act, PAIRS, body)

        @block.vector
        def _(v):
            s = Steps(v, steps)
            v.memset(k.zeros[:, :], 0.0).then_inc(wzero, 1)
            v.memset(k.W1e[:, :], 0.0).then_inc(wzero, 1)
            v.memset(k.W2e[:, :], 0.0).then_inc(wzero, 1)
            v.memset(k.W3e[:, :], 0.0).then_inc(wzero, 1)
            v.memset(k.X[96:P, LASTN:NB, :], 0.0).then_inc(wzero, 1)
            v.memset(k.b1z[:, :], 0.0).then_inc(wzero, 1)
            v.memset(k.ones[:, :], 1.0)
            v.wait_ge(l_c5, 16)
            v.tensor_copy(coarse5f[:, :], coarse5[:, :]).then_inc(c5_ready, 1)
            f = Steps(v, search)
            v.wait_ge(consts, 8)
            f.link(v.tensor_copy(nid[:, :], nid_i[:, :]))

            def nodes(c, q):
                f.link(copy_at(v, ncol[:, q], nid[:, bass.ds((2 * c + q) * GB, GB)]))

            def halves(g, q):
                v.tensor_scalar(nhalf[:, q], nid[:, bass.ds(g * GB, GB)], 0.5, None, ALU.add).then_inc(ncol_ready, 1)

            def rows_at(c, q):
                v.wait_ge(counted, GB * (2 * c + q + 1))
                f.link(v.tensor_scalar(rcount[:, q], rsum[:, q], 0.5, CR / 2 - 1.0, ALU.mult, ALU.add))
                f.link(v.tensor_scalar(rcount[:, q], rcount[:, q], 0.0, None, ALU.max))
                v.tensor_copy(row_i[:, q], rcount[:, q]).then_inc(row_ready, 1)

            def body(c, ahead):
                f.turn(BEFORE + PER * c)
                for q in range(2):
                    if ahead or q == 0:
                        rows_at(c + q, 1 - q)
                        halves(2 * c + q + 3, 1 - q)
                    v.wait_ge(row_got[q], 16 * GB * (c + 1))
                    for b in range(GB):
                        f.link(v.tensor_scalar(junk[:, 0:CC], rows[:, q, b, :], ncol[:, q, b:b + 1], 0.0, ALU.is_le,
                                               ALU.add, accum_out=rfound[:, q, b:b + 1]))
                    f.link(v.scalar_tensor_tensor(out=end_f[:, bass.ds((2 * c + q) * GB, GB)], in0=rcount[:, q],
                                                  scalar=float(CC), in1=rfound[:, q], op0=ALU.mult, op1=ALU.add))
                    if ahead:
                        nodes(c + 1, q)

            for q in range(2):
                halves(q, q)
                nodes(0, q)
            rows_at(0, 0)
            halves(2, 0)
            BEFORE = f.n
            PER = 2 * (2 + GB + 1 + 1)
            body(0, True)
            assert f.n == PER
            v.wait_ge(l_idx, 48)
            s.done(v.tensor_copy(dst_f[:, :], dst_i[:, :]))
            s.done(v.tensor_copy(k.src[:, 0:T], src_i[:, :]))
            s.done(v.memset(k.src[:, T:], 0.0))
            s.done(v.memset(k.same[:, T:], 0.0))
            s.done(v.memset(k.same[:, 0:1], 0.0))
            s.wait(1)
            s.done(v.tensor_tensor(k.same[:, 1:T], dst_f[:, 1:T], dst_f[:, 0:T - 1], ALU.is_equal))
            s.done(v.tensor_copy(cols[:, 0:1], dst_f[:, 0:1]))
            s.done(v.tensor_copy(cols[:, 1:2], dst_f[:, T - 1:T]))
            assert s.n == 8
            s.done(v.tensor_copy(k.firstf[:, :], dst_f[:, 0:1]))
            s.wait(s.n)
            s.done(v.scalar_tensor_tensor(out=k.rel_i[:, :], in0=k.src[:, 0:T], scalar=float(RELS), in1=typ_i[:, :],
                                   op0=ALU.mult, op1=ALU.add))
            s.done(v.tensor_copy(pid[:, :], pid_i[:, :]))
            s.wait(s.n)
            s.done(v.tensor_scalar(k.dump[:, 0:T], k.src[:, 0:T], -1.0, float(NP), ALU.mult, ALU.add))
            s.wait(s.n)
            s.link(v.tensor_scalar(k.dump[:, 0:T], k.dump[:, 0:T], pid[:, 0:1], None, ALU.add))
            s.done(v.memset(k.dump[:, T:], 0.0))
            with v.Fori(1, PAIRS - 1) as c:
                body(c, True)
            body(PAIRS - 1, False)
            s.done(v.tensor_scalar(fidx[:, :], cols[:, 0:1], 1.0, None, ALU.add))
            v.tensor_copy(end_i[:, :], end_f[:, :]).then_inc(end_ready, 1)
            s.link(v.tensor_scalar(tmp[:, :], end_f[:, :], -1.0, 0.0, ALU.add, ALU.max))
            s.done(v.memset(k.last_i[:, NB:], 0))
            s.done(v.tensor_copy(k.last_i[:, 0:NB], tmp[:, :]))
            v.wait_ge(ends_moved, 48)
            s.link(v.tensor_copy(start_f[:, :], start_i[:, :]))
            s.link(v.tensor_tensor(cnt[:, :], end_f[:, :], start_f[:, :], ALU.subtract))
            s.done(v.tensor_scalar(k.some[:, :], cnt[:, :], 0.5, None, ALU.is_gt))
            s.link(v.tensor_scalar(cnt[:, :], cnt[:, :], 1.0, None, ALU.max))
            s.link(v.reciprocal(k.rcnt[:, :], cnt[:, :]))
            s.link(v.tensor_scalar(cnt[:, :], nid[:, 0:NB], float(E), None, ALU.add))
            s.link(v.tensor_tensor(start_f[:, :], start_f[:, :], cnt[:, :], ALU.subtract))
            s.link(v.tensor_tensor(start_f[:, :], start_f[:, :], k.some[:, :], ALU.mult))
            s.link(v.tensor_tensor(cnt[:, :], start_f[:, :], cnt[:, :], ALU.add))
            s.done(v.tensor_copy(k.zrow_i[:, 0:NB], cnt[:, :]))
            v.wait_ge(fend_got, 16)
            s.link(v.tensor_copy(fend[:, :], fend_i[:, :]))
            s.link(v.tensor_scalar(cols[:, 2:3], pid[:, :], float(T), float(T), ALU.mult, ALU.add))
            s.link(v.tensor_tensor(cols[:, 2:3], fend[:, :], cols[:, 2:3], ALU.is_le))
            s.link(v.tensor_scalar(cols[:, 3:4], pid[:, :], float(E), None, ALU.add))
            s.link(v.tensor_scalar(fend[:, :], fend[:, :], -1.0, cols[:, 3:4], ALU.add, ALU.subtract))
            s.link(v.scalar_tensor_tensor(out=fend[:, :], in0=fend[:, :], scalar=cols[:, 2:3], in1=cols[:, 3:4],
                                          op0=ALU.mult, op1=ALU.add))
            s.done(v.tensor_copy(k.fix_i[:, :], fend[:, :]))
            v.wait_ge(rows_built, 1)
            s.done(v.tensor_scalar(k.before[:, :], psS, cols[:, 1:2], None, ALU.is_equal))
            s.link(v.tensor_copy(lastr[:, :], psL))
            s.link(v.tensor_copy(firstr[:, :], psF))
            for out, a in ((k.chain, lastr), (k.joins, firstr)):
                s.link(v.tensor_tensor(out[:, 1:P], a[:, 1:P], lastr[:, 0:P - 1], ALU.is_equal))
                s.link(v.memset(out[:, 0:1], 0.0))
                s.link(v.tensor_scalar(out[:, :], out[:, :], 1.0, HUGE, ALU.subtract, ALU.mult))


def edges_01(nc, k, ins):
    with ExitStack() as ctx:
        def sb(name, shape, dt=F32):
            return ctx.enter_context(nc.sbuf_tensor(name, shape, dt))

        def sem(name):
            return ctx.enter_context(nc.semaphore(name))

        v64 = sb("v64", [P, NS, SL, D])
        v16 = sb("v16", [P, NS, SL, A16])
        run = sb("run", [P, NS, SL, R1W])
        meta = sb("meta", [P, NS, 3, SL])
        mates = sb("mates", [P, 3, SL, P])
        later = sb("later", [P, 2, SL])
        route = sb("route", [P, 2, SL])
        row_i = sb("row_i1", [P, NS, SL], I32)
        sums = sb("sums", [P, NS, SL, D])
        loaded = [sem(f"loaded{q}") for q in range(NS)]
        stored = [sem(f"stored{q}") for q in range(NS)]
        added = [sem(f"added{q}") for q in range(NTAB)]
        meta_ready, spread, mates_ready, row_ready, run_ready, summed, sums_ready, vsteps = (
            sem(s) for s in ("meta_ready", "spread", "mates_ready", "row_ready1", "run_ready", "summed",
                             "sums_ready", "vsteps1"))
        e64 = ins["edge_attr_64"].rearrange("(p t) f -> p t f", p=P)
        e16 = ins["edge_attr_16"].rearrange("(p t) f -> p t f", p=P)
        R1 = k.R1[0:E, :].rearrange("(p t) f -> p t f", p=P)
        SLOTS = CHUNKS * NS

        def ps_spread(q):
            return k.psf[:, (q % 3) * 1024:(q % 3) * 1024 + SL * P]

        def ps_sum(q):
            return k.ps[:, 6 + q % 2, 0:SL * D]

        block = ctx.enter_context(nc.Block())

        @block.sync
        def _(sp):
            def load(c, q):
                at = c * CH + q * SL
                sp.dma_start(v64[:, q], e64[:, bass.ds(at, SL), :]).then_inc(loaded[q], 16)
                sp.dma_start(v16[:, q], e16[:, bass.ds(at, SL), :]).then_inc(loaded[q], 16)

            def store(c, q):
                sp.wait_ge(run_ready, NS * c + q + 1)
                sp.dma_start(R1[:, bass.ds(c * CH + q * SL, SL), :], run[:, q]).then_inc(stored[q], 16)

            for q in range(NS):
                load(0, q)
            with sp.Fori(0, CHUNKS - 1) as c:
                for q in range(NS):
                    store(c, q)
                    sp.wait_ge(summed, NS * c + q + 1)
                    load(c + 1, q)
            for q in range(NS):
                store(CHUNKS - 1, q)
            for q in range(NS):
                sp.wait_ge(stored[q], 16 * CHUNKS)

        @block.scalar
        def _(act):
            def copy_meta(c, q, at_first):
                if not at_first:
                    act.wait_ge(run_ready, NS * c + q + 1 - NS)
                    act.wait_ge(row_ready, NS * c + q + 1 - NS)
                at = c * CH + q * SL
                for j, a in enumerate((k.src, k.same, k.dump)):
                    last = act.copy(meta[:, q, j, :], a[:, bass.ds(at, SL)])
                    last.then_inc(meta_ready, 1)

            def body(c):
                for q in range(NS):
                    n = NS * c + q
                    copy_meta(c + (q + 1) // NS, (q + 1) % NS, is_first(c) and q < NS - 1)
                    act.wait_ge(summed, n + 1)
                    if not is_first(c):
                        act.wait_ge(added[NTAB - 1], 16 * (n - NS + 2))
                    act.copy(sums[:, q].rearrange("p t f -> p (t f)"), ps_sum(q)).then_inc(sums_ready, 1)

            copy_meta(0, 0, True)
            turns(act, CHUNKS, body)

        @block.tensor
        def _(pe):
            def spread_src(c, q, n, at_first):
                pe.wait_ge(meta_ready, 3 * n + 3)
                if not at_first:
                    pe.wait_ge(mates_ready, n - 1)
                ps = ps_spread(q)
                for t in range(SL):
                    nc.tensor.matmul(ps[:, t * P:(t + 1) * P], meta[:, q, 0, t:t + 1].to_broadcast([P, P]),
                                     k.ident[:, :], start=t in (0, 4), stop=False)
                nc.tensor.matmul(ps[:, 0:4 * P], k.ident[:, :],
                                 k.upper[:, :, :].rearrange("p a i -> p (a i)"), start=False, stop=True)
                nc.tensor.matmul(ps[:, 4 * P:5 * P], k.ident[:, :], k.upper[:, 0, :],
                                 start=False, stop=True).then_inc(spread, 1)

            def body(c):
                for q in range(NS):
                    n = NS * c + q
                    spread_src(c + (q + 1) // NS, (q + 1) % NS, n + 1, is_first(c) and q < 1)
                    pe.wait_ge(mates_ready, n + 1)
                    pe.wait_ge(loaded[q], 32 * c + 32)
                    if not (is_first(c) and q < 2):
                        pe.wait_ge(sums_ready, n - 1 if q else n)
                    for t in range(SL):
                        last = nc.tensor.matmul(ps_sum(q)[:, t * D:(t + 1) * D], mates[:, q % 3, t, :],
                                                v64[:, q, t, :], start=True, stop=True)
                    last.then_inc(summed, 1)

            spread_src(0, 0, 0, True)
            turns(pe, CHUNKS, body)

        @block.vector
        def _(v):
            s = Steps(v, vsteps)
            s.link(v.memset(run[:, NS - 1, SL - 1, :], 0.0))

            def body(c):
                s.turn(1 + PER * c)
                for q in range(NS):
                    n = NS * c + q
                    before = (q - 1) % NS

                    def sum_step(t):
                        p64 = run[:, q, t - 1, 0:D] if t else run[:, before, SL - 1, 0:D]
                        p16 = run[:, q, t - 1, D:] if t else run[:, before, SL - 1, D:]
                        s.done(v.scalar_tensor_tensor(out=run[:, q, t, 0:D], in0=p64, scalar=meta[:, q, 1, t:t + 1],
                                                      in1=v64[:, q, t, :], op0=ALU.mult, op1=ALU.add))
                        ins_ = v.scalar_tensor_tensor(out=run[:, q, t, D:], in0=p16, scalar=meta[:, q, 1, t:t + 1],
                                                      in1=v16[:, q, t, :], op0=ALU.mult, op1=ALU.add)
                        if t == SL - 1:
                            ins_.then_inc(run_ready, 1)
                            return None
                        return s.done(ins_)

                    v.wait_ge(spread, n + 1)
                    if not (is_first(c) and q < 2):
                        v.wait_ge(summed, n - 1)
                    v.tensor_tensor(mates[:, q % 3], ps_spread(q).rearrange("p (t i) -> p t i", t=SL),
                                    over(meta[:, q, 0, :], 2, P), ALU.is_equal).then_inc(mates_ready, 1)
                    v.wait_ge(loaded[q], 32 * c + 32)
                    if not is_first(c):
                        v.wait_ge(stored[q], 16 * c)
                    if q or not is_first(c):
                        v.wait_ge(run_ready, n)
                    prev = sum_step(0)
                    v.wait_ge(mates_ready, n + 1)
                    m1 = s.done(v.tensor_reduce(later[:, q % 2, :], mates[:, q % 3], AX.X, ALU.add))
                    s.wait(prev)
                    prev = sum_step(1)
                    s.wait(m1)
                    m2 = s.done(v.scalar_tensor_tensor(out=route[:, q % 2, :], in0=later[:, q % 2, :], scalar=1.5,
                                                       in1=meta[:, q, 2, :], op0=ALU.is_gt, op1=ALU.mult))
                    s.wait(prev)
                    prev = sum_step(2)
                    s.wait(m2)
                    if not is_first(c):
                        v.wait_ge(added[NTAB - 1], 16 * (n - NS + 2))
                    v.tensor_tensor(row_i[:, q, :], route[:, q % 2, :], meta[:, q, 0, :], ALU.add).then_inc(row_ready, 1)
                    for t in range(3, SL):
                        s.wait(prev)
                        prev = sum_step(t)

            PER = NS * (2 * SL + 1)
            turns(v, CHUNKS, body, s, PER)
            v.wait_ge(run_ready, SLOTS)
            v.tensor_copy(k.tail[:, :], run[:, NS - 1, SL - 1, :])

        @block.gpsimd
        def _(pool):
            def body(c):
                for q in range(NS):
                    n = NS * c + q
                    hold(pool, sums_ready, n + 1, k.passed)
                    hold(pool, row_ready, n + 1, k.passed)
                    for t in range(SL):
                        if not (is_first(c) and q == 0):
                            hold(pool, added[t], 16 * n, k.passed)
                        scatter(pool, k.tables[t], row_i[:, q, t:t + 1], sums[:, q, t, :], added[t], add=True)

            turns(pool, CHUNKS, body)
            for t in range(SL):
                pool.wait_ge(added[t], 16 * SLOTS)

    fix_rows(nc, k, 1, k.R1, R1W, False)


def fix_rows(nc, k, n, rows, width, maxima):
    with ExitStack() as ctx:
        def sb(name, shape, dt=F32):
            return ctx.enter_context(nc.sbuf_tensor(name, shape, dt))

        g = sb(f"fix_rows{n}", [P, width])
        lastT, runT, carT = (sb(f"{s}{n}", [MSG, P]) for s in ("fix_last", "fix_run", "fix_carry"))
        moved, pe_steps, v_steps = (ctx.enter_context(nc.semaphore(f"{s}{n}")) for s in ("fix_moved", "fix_pe", "fix_v"))
        sums = width // 2 if maxima else width
        psS, psT, psM = k.ps[:, 0, 0:sums], k.ps[0:MSG, 1, 0:P], k.ps[:, 2, 0:MSG]
        ready = 6 if maxima else 1

        block = ctx.enter_context(nc.Block())

        @block.gpsimd
        def _(pool):
            gather(pool, g[:, :], rows, k.fix_i[:, :], moved)
            pool.wait_ge(v_steps, ready)
            scatter(pool, rows, k.fix_i[:, :], g[:, :], moved)
            pool.wait_ge(moved, 32)

        @block.tensor
        def _(pe):
            nc.tensor.matmul(psS, k.before[:, :], k.tail[:, 0:sums], start=True, stop=True).then_inc(pe_steps, 1)
            if maxima:
                nc.tensor.transpose(psT, k.tail[:, sums:width], k.ident[:, :]).then_inc(pe_steps, 1)
                pe.wait_ge(v_steps, 5)
                nc.tensor.transpose(psM, carT[:, :], k.ident[0:MSG, 0:MSG]).then_inc(pe_steps, 1)

        @block.vector
        def _(v):
            s = Steps(v, v_steps)
            v.wait_ge(moved, 16)
            v.wait_ge(pe_steps, 1)
            s.link(v.tensor_tensor(g[:, 0:sums], g[:, 0:sums], psS, ALU.add))
            if maxima:
                v.wait_ge(pe_steps, 2)
                s.link(v.tensor_copy(lastT[:, :], psT))
                s.link(v.tensor_tensor_scan(out=runT[:, :], data0=k.chain[:, :], data1=lastT[:, :], initial=0.0,
                                            op0=ALU.add, op1=ALU.max))
                s.link(v.memset(carT[:, 0:1], -HUGE))
                s.link(v.tensor_tensor(carT[:, 1:P], runT[:, 0:P - 1], k.joins[:, 1:P], ALU.add))
                v.wait_ge(pe_steps, 3)
                s.done(v.tensor_tensor(g[:, sums:], g[:, sums:], psM, ALU.max))


def norm(v, s, y, x_out, st, sq, std_in, std, eng_wait, act_sem, done=None):
    s.link(v.tensor_reduce(st[:, 0, :], y, AX.X, ALU.add))
    s.link(v.tensor_scalar(st[:, 0, :], st[:, 0, :], 1.0 / D, None, ALU.mult))
    s.link(v.tensor_tensor(y, y, over(st[:, 0, :], 2, D), ALU.subtract))
    s.link(v.tensor_tensor(sq, y, y, ALU.mult))
    s.link(v.tensor_reduce(st[:, 1, :], sq, AX.X, ALU.add))
    v.tensor_scalar(std_in, st[:, 1, :], 1.0 / D, EPS, ALU.mult, ALU.add).then_inc(act_sem, 1)
    eng_wait()
    s.link(v.reciprocal(st[:, 2, :], std))
    last = v.tensor_tensor(x_out, y, over(st[:, 2, :], 2, D), ALU.mult)
    if done is None:
        s.link(last)
    else:
        last.then_inc(done, 1)


def nodes_01(nc, k, ins):
    with ExitStack() as ctx:
        def sb(name, shape, dt=F32):
            return ctx.enter_context(nc.sbuf_tensor(name, shape, dt))

        def sem(name):
            return ctx.enter_context(nc.semaphore(name))

        tabs = sb("tabs", [P, 2, NTAB, GB * D])
        got = sb("got", [P, 2, GB, R1W])
        idx = sb("idx", [P, 2, GB], I32)
        cat = sb("cat", [P, 2, GB, HID])
        cat1 = sb("cat1", [P, 2, GB, R1W])
        catT = sb("catT", [P, GB * P])
        hT = sb("hT", [P, GB * P])
        y = sb("y", [P, GB, D])
        sq = sb("sq", [P, GB, D])
        st = sb("st", [P, 3, GB])
        std_in = sb("std_in", [P, GB])
        std = sb("std", [P, GB])
        x2 = sb("x2", [P, 2, GB, 2, D])
        x2T, rest = sb("x2T", [P, GB * P]), sb("rest", [P, GB * P])
        xm = sb("xm", [D, GB * P], BF16)
        x_hm, x_lh = sb("x_hm", [P, 2, GB * P], BF16), sb("x_lh", [P, 2, GB * P], BF16)
        w_hh, w_mm, w_hl = (sb(s, [P, RELS * D], BF16) for s in ("w_hh", "w_mm", "w_hl"))
        w_rest = sb("w_rest", [P, RELS * D])
        tab = sb("tab", [P, GB, RELS * D])
        ub = sb("ub", [P, 1])
        tabs_got = [sem(f"tabs_got{q}") for q in range(2)]
        rows_got = [sem(f"rows_got{q}") for q in range(2)]
        tab_put = [sem(f"tab_put{q}") for q in range(2)]
        (idx_ready, agg_ready, cat_ready, turned, turned_c, hid, hid_r, outp, vsteps, var, root, x_new, x2T_ready, xh_ready,
         parts_ready, tab_made,
         tab_ready, ubs, ub_ready) = (
            sem(s) for s in ("idx_ready", "agg_ready", "cat_ready", "turned", "turned_c", "hid", "hid_r", "outp", "nsteps", "var",
                             "root", "x_new", "x2T_ready", "xh_ready", "parts_ready", "tab_made", "tab_ready", "ubs", "ub_ready"))
        Y = k.Y.rearrange("(p b r) f -> p b (r f)", p=P, b=NB)
        psT = psH = k.psf[:, 0:GB * P]
        psY = k.ps[:, 2, 0:GB * D]
        psR = [k.psf[:, 2048:3072], k.psf[:, 3072:4096]]
        halves = ((0, 512), (512, GB * P))
        PARTS = ((0, 3), (3, GB))

        def later(c, q):
            return not is_first(c) or q > 0

        block = ctx.enter_context(nc.Block())

        @block.sync
        def _(sp):
            def load(c, q):
                for t in range(NTAB):
                    sp.dma_start(tabs[:, q, t, :],
                                 k.tables[t][0:NP, :].rearrange("(p b) f -> p (b f)", p=P)
                                 [:, bass.ds((2 * c + q) * GB * D, GB * D)]).then_inc(tabs_got[q], 16)

            def save(g, b, c, q):
                sp.wait_ge(tab_ready, g * GB + b + 1)
                sp.dma_start(Y[:, bass.ds(g * GB + b, 1), :], tab[:, b, None, :]).then_inc(tab_put[q], 16)

            def body(c, ahead):
                for q in range(2):
                    if ahead:
                        sp.wait_ge(idx_ready, 2 * c + q + 3)
                        load(c + 1, q)
                    if later(c, q):
                        for b in range(GB):
                            save(2 * c + q - 1, b, c, 1 - q)

            for q in range(2):
                load(0, q)
            turns_ahead(sp, PAIRS, body)
            for b in range(GB):
                save(2 * PAIRS - 1, b, PAIRS - 1, 1)
            for q in range(2):
                sp.wait_ge(tab_put[q], 16 * PAIRS * GB)

        @block.gpsimd
        def _(pool):
            def body(c):
                for q in range(2):
                    hold(pool, idx_ready, 2 * c + q + 1, k.passed)
                    for b in range(GB):
                        gather(pool, got[:, q, b, :], k.R1, idx[:, q, b:b + 1], rows_got[q])

            turns(pool, PAIRS, body)

        @block.tensor
        def _(pe):
            nc.tensor.matmul(k.ps[:, 3, 0:1], k.W1bu[:, :], k.u1[:, :], start=True, stop=True).then_inc(ubs, 1)

            def mlp(step, ready, n, src, w, W1, W2, b2):
                pe.wait_ge(ready, n)
                for a, z in halves:
                    for b in range(a // P, z // P):
                        last = nc.tensor.transpose(psT[0:w, b * P:(b + 1) * P], src[:, b, :], k.ident[:, :])
                    last.then_inc(turned, 1)
                for i, (a, z) in enumerate(halves):
                    pe.wait_ge(turned_c, 2 * step + i + 1)
                    nc.tensor.matmul(psH[:, a:z], W1, catT[0:w, a:z], start=True, stop=True).then_inc(hid, 1)
                nc.tensor.matmul(psY, k.ones[0:1, :], over(b2, 1, GB), start=True, stop=False)
                for i, (a, z) in enumerate(halves):
                    pe.wait_ge(hid_r, 2 * step + i + 1)
                    for b in range(a // P, z // P):
                        last = nc.tensor.matmul(psY[:, b * D:(b + 1) * D], hT[:, b * P:(b + 1) * P], W2,
                                                start=False, stop=b == GB - 1)
                last.then_inc(outp, 1)

            def table(g, x, part):
                hold(pe, parts_ready, g + 1, k.passed)
                for b in range(*part):
                    n = g * GB + b
                    if not (isinstance(g, int) and g == 0 and b < 2):
                        pe.wait_ge(tab_ready, n - 1)
                    m = (x * GB + b) % 2
                    cols = slice(b * P, (b + 1) * P)
                    for h in range(2):
                        half = slice(h * 512, (h + 1) * 512)
                        nc.tensor.matmul(psR[m][:, half], x_hm[:, x, cols], w_hh[:, half], start=True, stop=False)
                        nc.tensor.matmul(psR[m][:, half], x_hm[:, x, cols], w_mm[:, half], start=False, stop=False)
                        last = nc.tensor.matmul(psR[m][:, half], x_lh[:, x, cols], w_hl[:, half], start=False, stop=True)
                    last.then_inc(tab_made, 1)

            def body(c):
                for q in range(2):
                    g = 2 * c + q
                    mlp(2 * g, agg_ready, g + 1, cat[:, q], HID, k.W1a[:, :], k.W2a[:, :], k.b2a[0:1, :])
                    if later(c, q):
                        table(g - 1, 1 - q, PARTS[0])
                    mlp(2 * g + 1, cat_ready, g + 1, cat1[:, q], R1W, k.W1b[:, :], k.W2b[:, :], k.b2b[0:1, :])
                    if later(c, q):
                        table(g - 1, 1 - q, PARTS[1])
                    hold(pe, x_new, g + 1, k.passed)
                    for a, z in halves:
                        for b in range(a // P, z // P):
                            last = nc.tensor.transpose(psT[:, b * P:(b + 1) * P],
                                                       x2[:, q, b].rearrange("p a f -> p (a f)"), k.ident[:, :])
                        last.then_inc(turned, 1)
                    pe.wait_ge(x2T_ready, 2 * g + 2)

            turns(pe, PAIRS, body)
            for part in PARTS:
                table(2 * PAIRS - 1, 1, part)

        @block.scalar
        def _(act):
            def layer(c, q, l, w, bias):
                g = 2 * c + q
                step = 2 * g + l
                for i, (a, z) in enumerate(halves):
                    act.wait_ge(turned, 2 * (3 * g + l) + i + 1)
                    act.copy(catT[0:w, a:z], psT[0:w, a:z]).then_inc(turned_c, 1)
                for i, (a, z) in enumerate(halves):
                    act.wait_ge(hid, 2 * step + i + 1)
                    act.activation(hT[:, a:z], psH[:, a:z], ACT.Relu, bias=bias).then_inc(hid_r, 1)
                if later(c, q):
                    evacuate(g - 1, 1 - q, (PARTS[l][0], PARTS[l][0] + 2), c if q else c - 1)
                act.wait_ge(var, step + 1)
                act.activation(std[:, :], std_in[:, :], ACT.Sqrt).then_inc(root, 1)
                if later(c, q):
                    evacuate(g - 1, 1 - q, (PARTS[l][0] + 2, PARTS[l][1]), c if q else c - 1)

            def evacuate(g, x, part, c):
                for b in range(*part):
                    n, i = g * GB + b, x * GB + b
                    if b == 0 and not (isinstance(g, int) and g == 0):
                        act.wait_ge(tab_put[1 - x], 16 * GB * (c + x))
                    act.wait_ge(tab_made, n + 1)
                    act.copy(tab[:, b, :], psR[i % 2]).then_inc(tab_ready, 1)

            def body(c):
                for q in range(2):
                    g = 2 * c + q
                    layer(c, q, 0, HID, k.b1a[:, 0:1])
                    layer(c, q, 1, R1W, ub[:, 0:1])
                    if later(c, q):
                        act.wait_ge(parts_ready, g)
                    for i, (a, z) in enumerate(halves):
                        act.wait_ge(turned, 2 * (3 * g + 2) + i + 1)
                        act.copy(x2T[:, a:z], psT[:, a:z]).then_inc(x2T_ready, 1)
                    act.wait_ge(x2T_ready, 2 * g + 2)
                    act.copy(x_hm[:, q], x2T[:, :]).then_inc(xh_ready, 1)
                    act.copy(x_lh[D:, q], x2T[D:, :]).then_inc(xh_ready, 1)

            act.wait_ge(ubs, 1)
            act.activation(ub[:, :], k.ps[:, 3, 0:1], ACT.Identity, bias=k.b1b[:, 0:1]).then_inc(ub_ready, 1)
            act.wait_ge(ub_ready, 1)
            turns(act, PAIRS, body)
            for part in PARTS:
                evacuate(2 * PAIRS - 1, 1, part, PAIRS - 1)

        @block.vector
        def _(v):
            s = Steps(v, vsteps)

            def next_idx(c, q):
                copy_at(v, idx[:, q], k.last_i[:, bass.ds((2 * c + q) * GB, GB)]).then_inc(idx_ready, 1)

            def aggregate(c, q):
                blk = bass.ds((2 * c + q) * GB, GB)
                v.wait_ge(rows_got[q], 16 * GB * (c + 1))
                v.wait_ge(tabs_got[q], 16 * NTAB * (c + 1))
                s.link(v.tensor_tensor(cat1[:, q], got[:, q], over(k.some[:, blk], 2, R1W), ALU.mult))
                agg = cat[:, q, :, D:]
                for t in range(NTAB):
                    tt = tabs[:, q, t, :].rearrange("p (b f) -> p b f", b=GB)
                    s.link(v.tensor_tensor(agg, cat1[:, q, :, 0:D] if t == 0 else agg, tt, ALU.add))
                s.link(v.tensor_tensor(cat1[:, q, :, D:], cat1[:, q, :, D:], over(k.rcnt[:, blk], 2, A16), ALU.mult))
                copy_at(v, cat[:, q, :, 0:D], k.X[:, blk, :]).then_inc(agg_ready, 1)
                next_idx(c + 1, q)

            def layer(g, src, out, done):
                v.wait_ge(outp, g + 1)
                s.link(v.tensor_tensor(y[:, :, :], psY.rearrange("p (b f) -> p b f", b=GB), src, ALU.add))
                norm(v, s, y[:, :, :], out, st, sq[:, :, :], std_in[:, :], std[:, :],
                     lambda: v.wait_ge(root, g + 1), var, done)

            def body(c, ahead):
                s.turn(BEFORE + PER * c)
                for q in range(2):
                    g = 2 * c + q
                    layer(2 * g, cat[:, q, :, 0:D], cat1[:, q, :, 0:D], cat_ready)
                    if ahead or q == 0:
                        aggregate(c + q, 1 - q)
                    layer(2 * g + 1, cat1[:, q, :, 0:D], x2[:, q, :, 0, :], None)
                    copy_at(v, x2[:, q, :, 1, :], x2[:, q, :, 0, :]).then_inc(x_new, 1)
                    s.done(copy_at(v, k.X[:, bass.ds(g * GB, GB), :], x2[:, q, :, 0, :]))
                    v.wait_ge(xh_ready, 2 * g + 2)
                    s.link(v.tensor_tensor(rest[:, :], x2T[:, :], x_hm[:, q], ALU.subtract))
                    s.done(v.tensor_copy(x_hm[D:, q], rest[D:, :]))
                    s.link(v.tensor_copy(xm[:, :], rest[0:D, :]))
                    v.tensor_tensor(x_lh[0:D, q], rest[0:D, :], xm[:, :], ALU.subtract).then_inc(parts_ready, 1)

            for q in range(2):
                next_idx(0, q)
            w = k.W2r[:, :, :].rearrange("i r o -> i (r o)")
            s.done(v.tensor_copy(w_hl[0:D, :], w[0:D, :]))
            s.link(v.tensor_copy(w_hh[:, :], w))
            s.link(v.tensor_tensor(w_rest[:, :], w, w_hh[:, :], ALU.subtract))
            s.link(v.tensor_copy(w_mm[:, :], w_rest[:, :]))
            s.done(v.tensor_tensor(w_hl[D:, :], w_rest[D:, :], w_mm[D:, :], ALU.subtract))
            aggregate(0, 0)
            BEFORE = s.n
            PER = 2 * (NTAB + 2 + 7 + 8 + 1 + 3)
            turns_ahead(v, PAIRS, body, s, PER)


def edges_2(nc, k, ins):
    with ExitStack() as ctx:
        def sb(name, shape, dt=F32):
            return ctx.enter_context(nc.sbuf_tensor(name, shape, dt))

        def sem(name):
            return ctx.enter_context(nc.semaphore(name))

        msg = sb("msg", [P, NS, SL, D])
        run = sb("run2", [P, NS, SL, D])
        idx = sb("idx2", [P, NS, SL], I32)
        same = sb("same2", [P, NS, SL])
        got = [sem(f"msg_got{q}") for q in range(NS)]
        stored = [sem(f"stored2_{q}") for q in range(NS)]
        meta_ready, run_ready, vsteps, zero_put = (
            sem(s) for s in ("meta_ready2", "run_ready2", "vsteps2", "zero_put2"))
        R2 = k.R2[0:E, :].rearrange("(p t) f -> p t f", p=P)
        Z = k.Z[0:E, :].rearrange("(p t) f -> p (t f)", p=P)

        block = ctx.enter_context(nc.Block())

        @block.sync
        def _(sp):
            def body(c):
                for q in range(NS):
                    sp.wait_ge(run_ready, NS * c + q + 1)
                    sp.dma_start(R2[:, bass.ds(c * CH + q * SL, SL), :], run[:, q]).then_inc(stored[q], 16)
                sp.dma_start(Z[:, bass.ds(c * CH * MSG, CH * MSG)], k.zeros[:, 0:CH * MSG]).then_inc(zero_put, 16)

            turns(sp, CHUNKS, body)
            for q in range(NS):
                sp.wait_ge(stored[q], 16 * CHUNKS)
            sp.wait_ge(zero_put, 16 * CHUNKS)

        @block.scalar
        def _(act):
            def body(c):
                for q in range(NS):
                    if not is_first(c):
                        act.wait_ge(run_ready, NS * c + q + 1 - NS)
                    at = bass.ds(c * CH + q * SL, SL)
                    act.copy(idx[:, q], k.rel_i[:, at]).then_inc(meta_ready, 1)
                    act.copy(same[:, q], k.same[:, at]).then_inc(meta_ready, 1)

            turns(act, CHUNKS, body)

        @block.gpsimd
        def _(pool):
            def body(c):
                for q in range(NS):
                    hold(pool, meta_ready, 2 * (NS * c + q + 1), k.passed)
                    for t in range(SL):
                        gather(pool, msg[:, q, t, :], k.Y, idx[:, q, t:t + 1], got[q])

            turns(pool, CHUNKS, body)

        @block.vector
        def _(v):
            s = Steps(v, vsteps)
            s.link(v.memset(run[:, NS - 1, SL - 1, :], 0.0))

            def body(c):
                s.turn(1 + PER * c)
                for q in range(NS):
                    v.wait_ge(got[q], 16 * SL * (c + 1))
                    if not is_first(c):
                        v.wait_ge(stored[q], 16 * c)
                    for t in range(SL):
                        prev = run[:, q, t - 1, :] if t else run[:, (q - 1) % NS, SL - 1, :]
                        if t:
                            s.wait(s.n)
                        elif q or not is_first(c):
                            v.wait_ge(run_ready, NS * c + q)
                        ins_ = v.scalar_tensor_tensor(out=run[:, q, t, :], in0=prev, scalar=same[:, q, t:t + 1],
                                                      in1=msg[:, q, t, :], op0=ALU.mult, op1=ALU.add)
                        if t == SL - 1:
                            ins_.then_inc(run_ready, 1)
                        else:
                            s.done(ins_)

            PER = NS * (SL - 1)
            turns(v, CHUNKS, body, s, PER)
            v.wait_ge(run_ready, CHUNKS * NS)
            v.tensor_copy(k.tail[:, 0:D], run[:, NS - 1, SL - 1, :])

    fix_rows(nc, k, 2, k.R2, D, False)


def nodes_2(nc, k, ins):
    with ExitStack() as ctx:
        def sb(name, shape, dt=F32):
            return ctx.enter_context(nc.sbuf_tensor(name, shape, dt))

        def sem(name):
            return ctx.enter_context(nc.semaphore(name))

        got = sb("got2", [P, 2, GB, D])
        idx = sb("nidx2", [P, 2, GB], I32)
        zidx = sb("zidx", [P, 2, GB], I32)
        y = sb("y2", [P, GB, D])
        sq = sb("sq2", [P, GB, D])
        st = sb("st2", [P, 3, GB])
        std_in = sb("std_in2", [P, GB])
        std = sb("std2", [P, GB])
        x3 = sb("x3", [P, 2, GB, D])
        x3T = sb("x3T", [D, GB * P])
        yz = sb("yz", [P, 2, GB, D])
        first_i = sb("first_i", [P, 1], I32)
        rows_got = [sem(f"rows_got2{q}") for q in range(2)]
        z_put = [sem(f"z_put{q}") for q in range(2)]
        yz_put = [sem(f"yz_put{q}") for q in range(2)]
        idx_ready, zidx_ready, x_ready, turned, turned_c, outp, vsteps, var, root, yz_ready, zi = (
            sem(s) for s in ("idx_ready2", "zidx_ready", "x_ready", "turned2", "turned_c2", "outp2", "nsteps2", "var2",
                             "root2", "yz_ready", "zinit_got"))
        psT, psY = k.psf[0:D, 0:GB * P], k.ps[:, 4, 0:GB * D]
        ytab = k.ytab.rearrange("(p b) f -> p b f", p=P)
        ztab = k.ztab.rearrange("(p b) f -> p b f", p=P)

        block = ctx.enter_context(nc.Block())

        @block.sync
        def _(sp):
            def body(c):
                for q in range(2):
                    g = 2 * c + q
                    sp.wait_ge(yz_ready, g + 1)
                    sp.dma_start(ytab[:, bass.ds(g * GB, GB), :], yz[:, q, :, 0:MSG]).then_inc(yz_put[q], 16)
                    sp.dma_start(ztab[:, bass.ds(g * GB, GB), :], yz[:, q, :, MSG:]).then_inc(yz_put[q], 16)

            turns(sp, PAIRS, body)
            for q in range(2):
                sp.wait_ge(yz_put[q], 32 * PAIRS)

        @block.gpsimd
        def _(pool):
            def fetch(c, q):
                hold(pool, idx_ready, 2 * c + q + 1, k.passed)
                for b in range(GB):
                    gather(pool, got[:, q, b, :], k.R2, idx[:, q, b:b + 1], rows_got[q])

            def body(c, ahead):
                for q in range(2):
                    if ahead:
                        fetch(c + 1, q)
                    hold(pool, yz_ready, 2 * c + q + 1, k.passed)
                    hold(pool, zidx_ready, 2 * c + q + 1, k.passed)
                    for b in range(GB):
                        scatter(pool, k.Z, zidx[:, q, b:b + 1], yz[:, q, b, MSG:], z_put[q])

            for q in range(2):
                fetch(0, q)
            turns_ahead(pool, PAIRS, body)
            for q in range(2):
                pool.wait_ge(z_put[q], 16 * GB * PAIRS)
                pool.wait_ge(yz_put[q], 32 * PAIRS)
            pool.wait_ge(zidx_ready, 2 * PAIRS + 1)
            gather(pool, k.zinit[:, :], k.ztab, first_i[:, :], zi)
            pool.wait_ge(zi, 16)

        @block.tensor
        def _(pe):
            def body(c):
                for q in range(2):
                    g = 2 * c + q
                    hold(pe, x_ready, g + 1, k.passed)
                    for b in range(GB):
                        last = nc.tensor.transpose(psT[:, b * P:(b + 1) * P], x3[:, q, b, :], k.ident[:, :])
                    last.then_inc(turned, 1)
                    if not (is_first(c) and q == 0):
                        pe.wait_ge(yz_ready, g)
                    nc.tensor.matmul(psY, k.ones[0:1, :], over(k.b1z[0:1, :], 1, GB), start=True, stop=False)
                    pe.wait_ge(turned_c, g + 1)
                    for b in range(GB):
                        last = nc.tensor.matmul(psY[:, b * D:(b + 1) * D], x3T[:, b * P:(b + 1) * P], k.Wyz[:, :],
                                                start=False, stop=b == GB - 1)
                    last.then_inc(outp, 1)

            turns(pe, PAIRS, body)

        @block.scalar
        def _(act):
            def body(c):
                for q in range(2):
                    g = 2 * c + q
                    act.wait_ge(var, g + 1)
                    act.activation(std[:, :], std_in[:, :], ACT.Sqrt).then_inc(root, 1)
                    act.wait_ge(turned, g + 1)
                    act.copy(x3T[:, :], psT).then_inc(turned_c, 1)
                    act.wait_ge(outp, g + 1)
                    if not is_first(c):
                        act.wait_ge(yz_put[q], 32 * c)
                        act.wait_ge(z_put[q], 16 * GB * c)
                    act.copy(yz[:, q].rearrange("p b f -> p (b f)"), psY).then_inc(yz_ready, 1)

            turns(act, PAIRS, body)

        @block.vector
        def _(v):
            s = Steps(v, vsteps)

            def next_idx(c, q):
                copy_at(v, idx[:, q], k.last_i[:, bass.ds((2 * c + q) * GB, GB)]).then_inc(idx_ready, 1)

            def body(c):
                s.turn(PER * c)
                for q in range(2):
                    g = 2 * c + q
                    blk = bass.ds(g * GB, GB)
                    v.wait_ge(rows_got[q], 16 * GB * (c + 1))
                    s.link(v.tensor_tensor(y[:, :, :], got[:, q], over(k.some[:, blk], 2, D), ALU.mult))
                    next_idx(c + 1, q)
                    s.link(v.tensor_tensor(y[:, :, :], y[:, :, :], k.X[:, blk, :], ALU.add))
                    if not is_first(c):
                        v.wait_ge(turned, g - 1)
                    norm(v, s, y[:, :, :], x3[:, q], st, sq[:, :, :], std_in[:, :], std[:, :],
                         lambda: v.wait_ge(root, g + 1), var)
                    copy_at(v, k.X[:, blk, :], x3[:, q]).then_inc(x_ready, 1)
                    if not is_first(c):
                        v.wait_ge(z_put[q], 16 * GB * c)
                    copy_at(v, zidx[:, q], k.zrow_i[:, blk]).then_inc(zidx_ready, 1)

            for q in range(2):
                next_idx(0, q)
            PER = 2 * (2 + 7)
            turns(v, PAIRS, body, s, PER)
            v.tensor_copy(first_i[:, :], k.firstf[:, :]).then_inc(zidx_ready, 1)


def edges_3(nc, k, ins):
    with ExitStack() as ctx:
        def sb(name, shape, dt=F32):
            return ctx.enter_context(nc.sbuf_tensor(name, shape, dt))

        def sem(name):
            return ctx.enter_context(nc.semaphore(name))

        W = SL3 * MSG
        ea = sb("ea", [P, NS3, W])
        zs = sb("zs", [P, NS3, W])
        zx = sb("zx", [P, NS3, W])
        yg = sb("yg", [P, NS3, W])
        run = sb("run3", [P, NS3, SL3, 2 * MSG])
        eaT = sb("eaT", [P, LANES, W])
        h1 = sb("h1", [P, LANES, W])
        h2 = sb("h2", [P, LANES, W])
        idx = sb("idx3", [P, NS3, SL3], I32)
        same = sb("same3", [P, NS3, SL3])
        anew = sb("anew", [P, NS3, SL3])
        loaded = [sem(f"loaded3{q}") for q in range(NS3)]
        got = [sem(f"y_got{q}") for q in range(NS3)]
        stored = [sem(f"stored3{q}") for q in range(NS3)]
        idx_ready, turned, turned_c, pre, pre_r, mid, mid_r, fin, zready, run_ready, vsteps = (
            sem(s) for s in ("idx_ready3e", "turned3", "turned_c3", "pre", "pre_r", "mid", "mid_r", "fin", "zready",
                             "run_ready3", "vsteps3"))
        e32 = ins["edge_attr_32"].rearrange("(p t) f -> p (t f)", p=P)
        Z = k.Z[0:E, :].rearrange("(p t) f -> p (t f)", p=P)
        R3 = k.R3[0:E, :].rearrange("(p t) f -> p t f", p=P)
        LAST = CHUNKS3 - 1

        def ps(stage, q):
            return k.ps[:, LANES * stage + q % LANES, 0:W]

        def groups(steps):
            return [(4 * MSG * g, min(4, steps - 4 * g) * MSG) for g in range(-(-steps // 4))]

        def cuts(steps):
            return [(0, W, P)] if steps == SL3 else [(a, a + P, w) for a, w in groups(steps)]

        def lags(c, q, n):
            return not is_first(c) or q >= n

        block = ctx.enter_context(nc.Block())

        @block.sync
        def _(sp):
            def load(c, q, steps=SL3):
                at = bass.ds((c * CH3 + q * SL3) * MSG, steps * MSG)
                sp.dma_start(ea[:, q, 0:steps * MSG], e32[:, at]).then_inc(loaded[q], 16)
                sp.dma_start(zs[:, q, 0:steps * MSG], Z[:, at]).then_inc(loaded[q], 16)

            def store(c, q, steps=SL3):
                sp.wait_ge(run_ready, NS3 * c + q + 1)
                sp.dma_start(R3[:, bass.ds(c * CH3 + q * SL3, steps), :], run[:, q, 0:steps]).then_inc(stored[q], 16)

            def free(n):
                sp.wait_ge(turned, n + 1)
                sp.wait_ge(zready, n + 1)

            for q in range(NS3):
                load(0, q)
            with sp.Fori(0, LAST) as c:
                for q in range(NS3):
                    free(NS3 * c + q)
                    load(c + 1, q)
                    store(c, q)
            for q in range(NS3):
                if q < len(TAILS3):
                    free(NS3 * LAST + q)
                    load(CHUNKS3, q, TAILS3[q])
                store(LAST, q)
            for q, steps in enumerate(TAILS3):
                store(CHUNKS3, q, steps)
            for q in range(NS3):
                sp.wait_ge(stored[q], 16 * (CHUNKS3 + (q < len(TAILS3))))

        @block.gpsimd
        def _(pool):
            def slot(c, q, steps):
                hold(pool, idx_ready, NS3 * c + q + 1, k.passed)
                if not is_first(c):
                    hold(pool, pre, NS3 * c + q + 1 - NS3, k.passed)
                for t in range(steps):
                    gather(pool, yg[:, q, t * MSG:(t + 1) * MSG], k.ytab, idx[:, q, t:t + 1], got[q])

            def body(c):
                for q in range(NS3):
                    slot(c, q, SL3)

            turns(pool, CHUNKS3, body)
            for q, steps in enumerate(TAILS3):
                slot(CHUNKS3, q, steps)

        @block.tensor
        def _(pe):
            def slot(c, q, steps):
                n, m = NS3 * c + q, q % LANES
                behind = lags(c, q, LANES)
                pe.wait_ge(loaded[q], 32 * c + 32)
                if behind:
                    pe.wait_ge(turned_c, n + 1 - LANES)
                for a, w in groups(steps):
                    last = nc.tensor.transpose(ps(0, q)[0:w, a:a + P], ea[:, q, a:a + w], k.ident[:, :])
                last.then_inc(turned, 1)
                if behind:
                    pe.wait_ge(pre_r, n + 1 - LANES)
                pe.wait_ge(turned_c, n + 1)
                pe.wait_ge(zready, n + 1)
                pe.wait_ge(got[q], 16 * SL3 * c + 16 * steps)
                for a, b, w in cuts(steps):
                    nc.tensor.matmul(ps(1, q)[0:w, a:b], k.W1e[0:w, 0:w], eaT[0:w, m, a:b], start=True, stop=False)
                    for g, _ in groups(steps):
                        if a <= g < b:
                            nc.tensor.matmul(ps(1, q)[0:w, g:g + P], zx[:, q, g:g + w], k.ident[:, :],
                                             start=False, stop=False)
                            last = nc.tensor.matmul(ps(1, q)[0:w, g:g + P], yg[:, q, g:g + w], k.ident[:, :],
                                                    start=False, stop=g + P >= b)
                last.then_inc(pre, 1)
                if behind:
                    pe.wait_ge(mid_r, n + 1 - LANES)
                pe.wait_ge(pre_r, n + 1)
                for a, b, w in cuts(steps):
                    last = nc.tensor.matmul(ps(2, q)[0:w, a:b], k.W2e[0:w, 0:w], h1[0:w, m, a:b], start=True, stop=True)
                last.then_inc(mid, 1)
                if behind:
                    pe.wait_ge(run_ready, n + 1 - LANES)
                pe.wait_ge(mid_r, n + 1)
                for a, w in groups(steps):
                    last = nc.tensor.matmul(ps(3, q)[:, a:a + w], h2[0:w, m, a:a + P], k.W3e[0:w, 0:w],
                                            start=True, stop=True)
                last.then_inc(fin, 1)

            def body(c):
                for q in range(NS3):
                    slot(c, q, SL3)

            turns(pe, CHUNKS3, body)
            for q, steps in enumerate(TAILS3):
                slot(CHUNKS3, q, steps)

        @block.scalar
        def _(act):
            def copy_idx(c, q):
                act.copy(idx[:, q, :], k.src[:, bass.ds(c * CH3 + q * SL3, SL3)]).then_inc(idx_ready, 1)

            def slot(c, q, steps):
                n, m = NS3 * c + q, q % LANES
                behind = lags(c, q, LANES)
                act.wait_ge(turned, n + 1)
                if behind:
                    act.wait_ge(pre, n + 1 - LANES)
                for a, b, w in cuts(steps):
                    last = act.copy(eaT[0:w, m, a:b], ps(0, q)[0:w, a:b])
                last.then_inc(turned_c, 1)
                act.wait_ge(pre, n + 1)
                if behind:
                    act.wait_ge(mid, n + 1 - LANES)
                for a, b, w in cuts(steps):
                    last = act.activation(h1[0:w, m, a:b], ps(1, q)[0:w, a:b], ACT.Relu)
                last.then_inc(pre_r, 1)
                if steps == SL3 and not (isinstance(c, int) and c == CHUNKS3):
                    copy_idx(c + 1, q)
                act.wait_ge(mid, n + 1)
                if behind:
                    act.wait_ge(fin, n + 1 - LANES)
                for a, b, w in cuts(steps):
                    last = act.activation(h2[0:w, m, a:b], ps(2, q)[0:w, a:b], ACT.Relu, bias=k.b2e[0:w, 0:1])
                last.then_inc(mid_r, 1)

            def body(c):
                for q in range(NS3):
                    slot(c, q, SL3)

            for q in range(NS3):
                copy_idx(0, q)
            turns(act, CHUNKS3, body)
            for q, steps in enumerate(TAILS3):
                slot(CHUNKS3, q, steps)

        @block.vector
        def _(v):
            s = Steps(v, vsteps)
            s.link(v.memset(run[:, NS3 - 1, SL3 - 1, :], 0.0))

            def meta(c, q):
                at = bass.ds(c * CH3 + q * SL3, SL3)
                s.done(copy_at(v, same[:, q, :], k.same[:, at]))
                s.done(v.tensor_scalar(anew[:, q, :], k.same[:, at], 1.0, HUGE, ALU.subtract, ALU.mult))

            def spread_z(c, q, steps):
                n = NS3 * c + q
                v.wait_ge(loaded[q], 32 * c + 32)
                if not is_first(c):
                    v.wait_ge(pre, n + 1 - NS3)
                if lags(c, q, 1):
                    v.wait_ge(zready, n)
                for t in range(steps):
                    o = zx[:, q, t * MSG:(t + 1) * MSG]
                    if is_first(c) and q == 0 and t == 0:
                        last = v.tensor_copy(o, k.zinit[:, :])
                    else:
                        p = zx[:, q, (t - 1) * MSG:t * MSG] if t else zx[:, (q - 1) % NS3, W - MSG:]
                        last = v.scalar_tensor_tensor(out=o, in0=p, scalar=same[:, q, t:t + 1],
                                                      in1=zs[:, q, t * MSG:(t + 1) * MSG], op0=ALU.mult, op1=ALU.add)
                    if t < steps - 1:
                        s.link(last)
                    else:
                        last.then_inc(zready, 1)

            def aggregate(c, q, steps):
                n = NS3 * c + q
                v.wait_ge(fin, n + 1)
                if not is_first(c):
                    v.wait_ge(stored[q], 16 * c)
                if lags(c, q, 1):
                    v.wait_ge(run_ready, n)
                for t in range(steps):
                    h = ps(3, q)[:, t * MSG:(t + 1) * MSG]
                    p = run[:, q, t - 1, :] if t else run[:, (q - 1) % NS3, SL3 - 1, :]
                    s.done(v.scalar_tensor_tensor(out=run[:, q, t, 0:MSG], in0=p[:, 0:MSG], scalar=same[:, q, t:t + 1],
                                                  in1=h, op0=ALU.mult, op1=ALU.add))
                    b = v.scalar_tensor_tensor(out=run[:, q, t, MSG:], in0=p[:, MSG:], scalar=anew[:, q, t:t + 1],
                                               in1=h, op0=ALU.add, op1=ALU.max)
                    if t < steps - 1:
                        s.link(b)
                    else:
                        b.then_inc(run_ready, 1)

            def body(c):
                s.turn(BEFORE + PER * c)
                for q in range(NS3):
                    spread_z(c + (q + 1) // NS3, (q + 1) % NS3, SL3)
                    aggregate(c, q, SL3)
                    v.wait_ge(run_ready, NS3 * c + q + 1)
                    meta(c + 1, q)

            PER = NS3 * (3 * SL3 - 2 + 2)
            for q in range(NS3):
                meta(0, q)
            s.wait(s.n)
            spread_z(0, 0, SL3)
            BEFORE = s.n
            turns(v, CHUNKS3, body, s, PER)
            s.turn(BEFORE + PER * CHUNKS3)
            for q, steps in enumerate(TAILS3):
                if q + 1 < len(TAILS3):
                    spread_z(CHUNKS3, q + 1, TAILS3[q + 1])
                aggregate(CHUNKS3, q, steps)
            v.wait_ge(run_ready, CHUNKS3 * NS3 + len(TAILS3))
            v.tensor_copy(k.tail[:, 0:2 * MSG], run[:, len(TAILS3) - 1, TAILS3[-1] - 1, :])

    fix_rows(nc, k, 3, k.R3, 2 * MSG, True)


def nodes_3(nc, k, ins, out):
    with ExitStack() as ctx:
        def sb(name, shape, dt=F32):
            return ctx.enter_context(nc.sbuf_tensor(name, shape, dt))

        def sem(name):
            return ctx.enter_context(nc.semaphore(name))

        got = sb("got3", [P, 2, GB, 2 * MSG])
        idx = sb("nidx3", [P, 2, GB], I32)
        cat = sb("cat3", [P, 2, GB, HID])
        catT = sb("catT3", [P, GB * P])
        h1 = sb("nh1", [MSG, GB * P])
        h2 = sb("nh2", [MSG, GB * P])
        y = sb("y3", [P, GB, D])
        sq = sb("sq3", [P, GB, D])
        st = sb("st3", [P, 3, GB])
        std_in = sb("std_in3", [P, GB])
        std = sb("std3", [P, GB])
        ub = sb("ub3", [MSG, 1])
        rows_got = [sem(f"rows_got3{q}") for q in range(2)]
        idx_ready, cat_ready, turned, turned_c, hid, hid_r, hid2, hid2_r, outp, vsteps, var, root, ubs, ub_ready, y_ready, saved = (
            sem(s) for s in ("idx_ready3", "cat_ready3", "turned4", "turned_c4", "hid3", "hid_r3", "hid23", "hid2_r3",
                             "outp3", "nsteps3", "var3", "root3", "ubs3", "ub_ready3", "y_ready3", "saved"))
        psT, psH, psH2 = k.psf[:, 0:GB * P], k.psf[0:MSG, 1024:1024 + GB * P], k.psf[0:MSG, 2048:2048 + GB * P]
        psY = [k.ps[:, 6 + q, 0:GB * D] for q in range(2)]
        halves = ((0, 512), (512, GB * P))

        def later(c, q):
            return not is_first(c) or q > 0

        block = ctx.enter_context(nc.Block())

        @block.sync
        def _(sp):
            most = out[0:LASTP * NB, :].rearrange("(p b) f -> p b f", b=NB)
            rest = out[LASTP * NB:N, :].rearrange("(p b) f -> p b f", p=1)
            cuts = [0, PAIRS, 2 * PAIRS - 2, 2 * PAIRS]
            saves = 0
            for g0, g1 in zip(cuts, cuts[1:]):
                sp.wait_ge(y_ready, g1)
                a, z = g0 * GB, g1 * GB
                sp.dma_start(most[:, a:z, :], k.X[0:LASTP, a:z, :]).then_inc(saved, 16)
                saves += 1
                if a < LASTN:
                    z = min(z, LASTN)
                    sp.dma_start(rest[:, a:z, :], k.X[LASTP:LASTP + 1, a:z, :]).then_inc(saved, 16)
                    saves += 1
            sp.wait_ge(saved, 16 * saves)

        @block.gpsimd
        def _(pool):
            def body(c):
                for q in range(2):
                    hold(pool, idx_ready, 2 * c + q + 1, k.passed)
                    for b in range(GB):
                        gather(pool, got[:, q, b, :], k.R3, idx[:, q, b:b + 1], rows_got[q])

            turns(pool, PAIRS, body)

        @block.tensor
        def _(pe):
            nc.tensor.matmul(k.ps[0:MSG, 7, 0:1], k.W4u[:, :], k.u3[:, :], start=True, stop=True).then_inc(ubs, 1)

            def turn_rows(g, q):
                pe.wait_ge(cat_ready, g + 1)
                for a, z in halves:
                    for b in range(a // P, z // P):
                        last = nc.tensor.transpose(psT[:, b * P:(b + 1) * P], cat[:, q, b, :], k.ident[:, :])
                    last.then_inc(turned, 1)

            def output(g, q):
                if isinstance(g, int) and g < 2:
                    pe.wait_ge(ub_ready, 1)
                else:
                    pe.wait_ge(y_ready, g - 1)
                nc.tensor.matmul(psY[q], k.ones[0:1, :], over(k.b6[0:1, :], 1, GB), start=True, stop=False)
                hold(pe, hid2_r, g + 1, k.passed)
                for b in range(GB):
                    last = nc.tensor.matmul(psY[q][:, b * D:(b + 1) * D], h2[:, b * P:(b + 1) * P], k.W6[:, :],
                                            start=False, stop=b == GB - 1)
                last.then_inc(outp, 1)

            def body(c, ahead):
                for q in range(2):
                    g = 2 * c + q
                    for i, (a, z) in enumerate(halves):
                        pe.wait_ge(turned_c, 2 * g + i + 1)
                        nc.tensor.matmul(psH[:, a:z], k.W4a[:, :], catT[:, a:z], start=True, stop=True).then_inc(hid, 1)
                    if later(c, q):
                        output(g - 1, 1 - q)
                    if ahead or q == 0:
                        turn_rows(g + 1, 1 - q)
                    hold(pe, hid_r, g + 1, k.passed)
                    for a, z in halves:
                        nc.tensor.matmul(psH2[:, a:z], k.W5[:, :], h1[:, a:z], start=True, stop=True).then_inc(hid2, 1)

            turn_rows(0, 0)
            turns_ahead(pe, PAIRS, body)
            output(2 * PAIRS - 1, 1)

        @block.scalar
        def _(act):
            def take_rows(g):
                for i, (a, z) in enumerate(halves):
                    act.wait_ge(turned, 2 * g + i + 1)
                    act.copy(catT[:, a:z], psT[:, a:z]).then_inc(turned_c, 1)

            def take_root(g):
                act.wait_ge(var, g + 1)
                act.activation(std[:, :], std_in[:, :], ACT.Sqrt).then_inc(root, 1)

            def body(c, ahead):
                for q in range(2):
                    g = 2 * c + q
                    for i, (a, z) in enumerate(halves):
                        act.wait_ge(hid, 2 * g + i + 1)
                        last = act.activation(h1[:, a:z], psH[:, a:z], ACT.Relu, bias=ub[:, 0:1])
                    last.then_inc(hid_r, 1)
                    if ahead or q == 0:
                        take_rows(g + 1)
                    for i, (a, z) in enumerate(halves):
                        act.wait_ge(hid2, 2 * g + i + 1)
                        last = act.activation(h2[:, a:z], psH2[:, a:z], ACT.Relu, bias=k.b5[:, 0:1])
                    last.then_inc(hid2_r, 1)
                    if later(c, q):
                        take_root(g - 1)

            act.wait_ge(ubs, 1)
            act.activation(ub[:, :], k.ps[0:MSG, 7, 0:1], ACT.Identity, bias=k.b4[:, 0:1]).then_inc(ub_ready, 1)
            act.wait_ge(ub_ready, 1)
            take_rows(0)
            turns_ahead(act, PAIRS, body)
            take_root(2 * PAIRS - 1)

        @block.vector
        def _(v):
            s = Steps(v, vsteps)

            def next_idx(c, q):
                copy_at(v, idx[:, q], k.last_i[:, bass.ds((2 * c + q) * GB, GB)]).then_inc(idx_ready, 1)

            def prepare(c, q):
                g = 2 * c + q
                blk = bass.ds(g * GB, GB)
                v.wait_ge(rows_got[q], 16 * GB * (c + 1))
                if not is_first(c):
                    v.wait_ge(turned, 2 * g - 2)
                ne = over(k.some[:, blk], 2, MSG)
                b3 = over(k.b3[:, :], 1, GB)
                mean, peak = cat[:, q, :, D:D + MSG], cat[:, q, :, D + MSG:]
                s.done(v.tensor_tensor(mean, got[:, q, :, 0:MSG], over(k.rcnt[:, blk], 2, MSG), ALU.mult))
                s.done(v.tensor_tensor(peak, got[:, q, :, MSG:], b3, ALU.add))
                s.wait(s.n)
                s.link(v.tensor_tensor(mean, mean, b3, ALU.add))
                s.done(v.tensor_tensor(mean, mean, ne, ALU.mult))
                s.done(v.tensor_tensor(peak, peak, ne, ALU.mult))
                copy_at(v, cat[:, q, :, 0:D], k.X[:, blk, :]).then_inc(cat_ready, 1)
                next_idx(c + 1, q)

            def update(g, q):
                blk = bass.ds(g * GB, GB)
                if not (isinstance(g, int) and g == 0):
                    v.wait_ge(y_ready, g)
                v.wait_ge(outp, g + 1)
                s.link(v.tensor_tensor(y[:, :, :], psY[q].rearrange("p (b f) -> p b f", b=GB), k.X[:, blk, :], ALU.add))
                norm(v, s, y[:, :, :], k.X[:, blk, :], st, sq[:, :, :], std_in[:, :], std[:, :],
                     lambda: v.wait_ge(root, g + 1), var, y_ready)

            PREPARE, UPDATE = 5, 7
            PER = 2 * (PREPARE + UPDATE)

            def body(c, ahead):
                if not is_first(c):
                    s.turn(PER * c + PREPARE - UPDATE)
                for q in range(2):
                    if ahead or q == 0:
                        prepare(c + q, 1 - q)
                    if later(c, q):
                        update(2 * c + q - 1, 1 - q)

            for q in range(2):
                next_idx(0, q)
            prepare(0, 0)
            turns_ahead(v, PAIRS, body)
            update(2 * PAIRS - 1, 1)


def build(nc, ins, out):
    with ExitStack() as ctx:
        k = Kernel()

        def sb(name, shape, dt=F32):
            return ctx.enter_context(nc.sbuf_tensor(name, shape, dt))

        def dram(name, shape, dt=F32):
            return nc.dram_tensor(name, shape, dt, kind="Internal").ap()

        k.ps = ctx.enter_context(nc.psum_tensor("ps", [P, 8, 512], F32))
        k.psf = k.ps[:, :, :].rearrange("p a b -> p (a b)")
        k.X = sb("X", [P, NB, D])
        k.some, k.rcnt = sb("some", [P, NB]), sb("rcnt", [P, NB])
        k.last_i, k.zrow_i = (sb(s, [P, NB + 2 * GB], I32) for s in ("last_i", "zrow_i"))
        k.src, k.same, k.dump = (sb(s, [P, T + CH]) for s in ("src_f", "same_f", "dump_f"))
        k.rel_i = sb("rel_i", [P, T], I32)
        k.firstf, k.fix_i, k.tail = sb("firstf", [P, 1]), sb("fix_i", [P, 1], I32), sb("tail", [P, R1W])
        k.before, k.chain, k.joins = sb("before", [P, P]), sb("chain", [MSG, P]), sb("joins", [MSG, P])
        k.zinit = sb("zinit", [P, MSG])
        k.ident, k.upper, k.ones = sb("ident", [P, P]), sb("upper", [P, 4, P]), sb("ones", [1, P])
        k.zeros = sb("zeros", [P, TABR * D // P // 4])
        k.W1a, k.W2a, k.b1a, k.b2a = sb("W1a", [HID, HID]), sb("W2a", [HID, D]), sb("b1a", [HID, 1]), sb("b2a", [1, D])
        k.W1b, k.W1bu, k.u1 = sb("W1b", [R1W, HID]), sb("W1bu", [D, HID]), sb("u1", [D, 1])
        k.W2b, k.b1b, k.b2b = sb("W2b", [HID, D]), sb("b1b", [HID, 1]), sb("b2b", [1, D])
        k.W2r = sb("W2r", [P, RELS, D])
        k.Wyz, k.b1z = sb("Wyz", [D, D]), sb("b1z", [1, D])
        k.W1e, k.W2e, k.W3e, k.b2e, k.b3 = (sb("W1e", [P, P]), sb("W2e", [P, P]), sb("W3e", [P, P]),
                                            sb("b2e", [P, 1]), sb("b3", [P, MSG]))
        k.W4a, k.W4u, k.u3, k.b4 = sb("W4a", [HID, MSG]), sb("W4u", [MSG, MSG]), sb("u3", [MSG, 1]), sb("b4", [MSG, 1])
        k.W5, k.b5, k.W6, k.b6 = sb("W5", [MSG, MSG]), sb("b5", [MSG, 1]), sb("W6", [MSG, D]), sb("b6", [1, D])

        def w(name, n=3):
            return ins[f"L{n}_gnn_{name}"]

        def col(a):
            return a.rearrange("(n a) -> n a", a=1)

        def row(a):
            return a.rearrange("(a n) -> a n", a=1)

        k.loads = [
            (k.W1a[:, :], w("W1", 0)), (k.W2a[:, :], w("W2", 0)), (k.b1a[:, :], col(w("b1", 0))), (k.b2a[:, :], row(w("b2", 0))),
            (k.W1b[:, :], w("W1", 1)[0:R1W, :]), (k.W1bu[:, :], w("W1", 1)[R1W:, :]), (k.u1[:, :], w("u", 1)[0:1, :].rearrange("a n -> n a")),
            (k.W2b[:, :], w("W2", 1)), (k.b1b[:, :], col(w("b1", 1))), (k.b2b[:, :], row(w("b2", 1))),
            (k.W2r[0:D, :, :], w("weight", 2).rearrange("r i o -> i r o")), (k.W2r[D:, :, :], w("weight", 2).rearrange("r i o -> i r o")),
            (k.Wyz[:, 0:MSG], w("W1")[0:D, :]), (k.Wyz[:, MSG:], w("W1")[D:2 * D, :]), (k.b1z[:, MSG:], row(w("b1"))),
            (k.b3[:, :], row(w("b3")).to_broadcast([P, MSG])),
            (k.W4a[:, :], w("W4")[0:HID, :]), (k.W4u[:, :], w("W4")[HID:, :]), (k.u3[:, :], w("u")[0:1, :].rearrange("a n -> n a")),
            (k.b4[:, :], col(w("b4"))), (k.W5[:, :], w("W5")), (k.b5[:, :], col(w("b5"))), (k.W6[:, :], w("W6")), (k.b6[:, :], row(w("b6"))),
        ]
        for j in range(4):
            d = slice(j * MSG, (j + 1) * MSG)
            k.loads += [(k.W1e[d, d], w("W1")[2 * D:, :]), (k.W2e[d, d], w("W2")), (k.W3e[d, d], w("W3")), (k.b2e[d, :], col(w("b2")))]

        k.coarse_d, k.ends = dram("coarse_d", [CR]), dram("ends", [NP + 1, 1], I32)
        k.tables = [dram(f"table{t}", [TABR, D]) for t in range(NTAB)]
        k.R1, k.R2, k.R3 = dram("R1", [E + P, R1W]), dram("R2", [E + P, D]), dram("R3", [E + P, 2 * MSG])
        k.Y = dram("Y", [NP * RELS, D])
        k.ytab, k.ztab, k.Z = dram("ytab", [NP, MSG]), dram("ztab", [NP, MSG]), dram("Z", [E + NP, MSG])

        k.passed = ctx.enter_context(nc.semaphore("passed"))
        setup(nc, k, ins)
        edges_01(nc, k, ins)
        nodes_01(nc, k, ins)
        edges_2(nc, k, ins)
        nodes_2(nc, k, ins)
        edges_3(nc, k, ins)
        nodes_3(nc, k, ins, out)


_INS = ['x', 'src', 'dst', 'edge_attr_16', 'edge_attr_32', 'edge_attr_64', 'edge_type_16',
        'L0_gnn_W1', 'L0_gnn_b1', 'L0_gnn_W2', 'L0_gnn_b2', 'L1_gnn_u', 'L1_gnn_W1', 'L1_gnn_b1', 'L1_gnn_W2',
        'L1_gnn_b2', 'L2_gnn_weight', 'L3_gnn_u', 'L3_gnn_W1', 'L3_gnn_b1', 'L3_gnn_W2', 'L3_gnn_b2', 'L3_gnn_W3',
        'L3_gnn_b3', 'L3_gnn_W4', 'L3_gnn_b4', 'L3_gnn_W5', 'L3_gnn_b5', 'L3_gnn_W6', 'L3_gnn_b6']


def kernel(**inputs):
    import numpy as np
    import concourse.bacc as bacc
    from concourse.bass_utils import run_bass_kernel_spmd

    nc = bacc.Bacc("TRN2", target_bir_lowering=False, num_devices=1)
    arrays, ins = {}, {}
    for name in _INS:
        a = np.ascontiguousarray(inputs[name])
        arrays[f"in_{name}"] = a
        ins[name] = nc.dram_tensor(f"in_{name}", a.shape, mybir.dt.from_np(a.dtype), kind="ExternalInput").ap()
    out = nc.dram_tensor("out", (N, D), F32, kind="ExternalOutput").ap()
    build(nc, ins, out)
    r = run_bass_kernel_spmd(nc, [arrays], core_ids=[0])
    return r.results[0]["out"]
```
